# Optimizing a Trainium2 kernel written in Bass

```python
import numpy as np
import jax
import jax.numpy as jnp

def _softmax(x, axis=-1):
    return jax.nn.softmax(x, axis=axis)

def _gelu(x):
    return jax.nn.gelu(x, approximate=True)

def _silu(x):
    return jax.nn.silu(x)

def _sigmoid(x):
    return jax.nn.sigmoid(x)

def _layernorm(x, axis=-1, eps=1e-05):
    m = jnp.mean(x, axis=axis, keepdims=True)
    v = jnp.var(x, axis=axis, keepdims=True)
    return (x - m) / jnp.sqrt(v + eps)

def _scatter_add(tgt, idx, src, axis=0):
    return tgt.at[idx].add(src)

def _segment_sum(src, seg, n):
    return jax.ops.segment_sum(src, seg, n)
kernel_name = 'mk_seq_preln_d1_jaxref_r8_4e1979'

def setup_inputs(seed: int=0):
    np.random.seed(seed)
    _w = jnp.asarray

    def _L0_attn_setup():
        import jax, jax.numpy as jnp
        import numpy as np
        B, T, C, H = (2, 256, 128, 16)
        key = jax.random.key(seed)
        ks = jax.random.split(key, 6)
        x = jax.random.normal(ks[0], (B, T, C), dtype=jnp.float32)
        wq = jax.random.normal(ks[1], (C, H * 3), dtype=jnp.float32) * C ** (-0.5)
        wk = jax.random.normal(ks[2], (C, H * 3), dtype=jnp.float32) * C ** (-0.5)
        wv = jax.random.normal(ks[3], (C, C), dtype=jnp.float32) * C ** (-0.5)
        wo = jax.random.normal(ks[4], (C, C), dtype=jnp.float32) * C ** (-0.5)
        dirs = jax.random.normal(ks[5], (H, 3), dtype=jnp.float32)
        head_dirs = dirs / jnp.linalg.norm(dirs, axis=1, keepdims=True)
        scale = jnp.full((1,), 1.0 / np.sqrt(3.0), dtype=jnp.float32)
        return {'x': x, 'wq': wq, 'wk': wk, 'wv': wv, 'wo': wo, 'head_dirs': head_dirs, 'scale': scale}
    _L0_attn_in = _L0_attn_setup()

    def _L0_ffn_setup():
        import jax, jax.numpy as jnp
        import numpy as np
        import math
        N_EMBD = 128
        HIDDEN = 4 * N_EMBD
        N_EXPERTS = 8
        TOP_K = 2
        B, T = (4, 256)

        def new_gelu(x):
            c = math.sqrt(2.0 / math.pi)
            return 0.5 * x * (1.0 + jnp.tanh(c * (x + 0.044715 * x * x * x)))

        def _moe_forward(x, Wfc_s, bfc_s, Wproj_s, bproj_s, Wr, Wfc, bfc, Wproj, bproj):
            Bb, Tt, C = x.shape
            xf = x.reshape(Bb * Tt, C)
            N = Bb * Tt
            shared = new_gelu(xf @ Wfc_s + bfc_s) @ Wproj_s + bproj_s
            logits = xf @ Wr
            probs = jax.nn.softmax(logits, axis=-1)
            topk_p, topk_i = jax.lax.top_k(probs, TOP_K)
            topk_p = topk_p / jnp.sum(topk_p, axis=-1, keepdims=True)
            gate = jnp.zeros((N, N_EXPERTS), dtype=xf.dtype)
            gate = gate.at[jnp.arange(N)[:, None], topk_i].add(topk_p)
            routed = jnp.zeros_like(xf)
            for e in range(N_EXPERTS):
                h = new_gelu(xf @ Wfc[e] + bfc[e]) @ Wproj[e] + bproj[e]
                routed = routed + h * gate[:, e:e + 1]
            return (shared + routed).reshape(Bb, Tt, C)
        key = jax.random.key(seed)
        ks = jax.random.split(key, 10)
        s = 0.02
        return {'x': jax.random.normal(ks[0], (B, T, N_EMBD), dtype=jnp.float32), 'Wfc_s': jax.random.normal(ks[1], (N_EMBD, HIDDEN), dtype=jnp.float32) * s, 'bfc_s': jnp.zeros((HIDDEN,), dtype=jnp.float32), 'Wproj_s': jax.random.normal(ks[2], (HIDDEN, N_EMBD), dtype=jnp.float32) * s, 'bproj_s': jnp.zeros((N_EMBD,), dtype=jnp.float32), 'Wr': jax.random.normal(ks[3], (N_EMBD, N_EXPERTS), dtype=jnp.float32) * s, 'Wfc': jax.random.normal(ks[4], (N_EXPERTS, N_EMBD, HIDDEN), dtype=jnp.float32) * s, 'bfc': jnp.zeros((N_EXPERTS, HIDDEN), dtype=jnp.float32), 'Wproj': jax.random.normal(ks[5], (N_EXPERTS, HIDDEN, N_EMBD), dtype=jnp.float32) * s, 'bproj': jnp.zeros((N_EXPERTS, N_EMBD), dtype=jnp.float32)}
    _L0_ffn_in = _L0_ffn_setup()
    _d = {'L0_attn_x': _L0_attn_in['x'], 'L0_attn_wq': _L0_attn_in['wq'], 'L0_attn_wk': _L0_attn_in['wk'], 'L0_attn_wv': _L0_attn_in['wv'], 'L0_attn_wo': _L0_attn_in['wo'], 'L0_attn_head_dirs': _L0_attn_in['head_dirs'], 'L0_attn_scale': _L0_attn_in['scale'], 'L0_ffn_Wfc_s': _L0_ffn_in['Wfc_s'], 'L0_ffn_bfc_s': _L0_ffn_in['bfc_s'], 'L0_ffn_Wproj_s': _L0_ffn_in['Wproj_s'], 'L0_ffn_bproj_s': _L0_ffn_in['bproj_s'], 'L0_ffn_Wr': _L0_ffn_in['Wr'], 'L0_ffn_Wfc': _L0_ffn_in['Wfc'], 'L0_ffn_bfc': _L0_ffn_in['bfc'], 'L0_ffn_Wproj': _L0_ffn_in['Wproj'], 'L0_ffn_bproj': _L0_ffn_in['bproj']}
    _x0 = _d['L0_attn_x']
    _d['L0_attn_x'] = jax.random.normal(jax.random.fold_in(jax.random.key(seed), 1), (8, 512, 128), dtype=_x0.dtype)
    del _x0
    return _d

def reference(L0_attn_x, L0_attn_wq, L0_attn_wk, L0_attn_wv, L0_attn_wo, L0_attn_head_dirs, L0_attn_scale, L0_ffn_Wfc_s, L0_ffn_bfc_s, L0_ffn_Wproj_s, L0_ffn_bproj_s, L0_ffn_Wr, L0_ffn_Wfc, L0_ffn_bfc, L0_ffn_Wproj, L0_ffn_bproj):

    def _L0_attn_ref(x, wq, wk, wv, wo, head_dirs, scale):
        import jax, jax.numpy as jnp
        import numpy as np
        B, T, C, H = (2, 256, 128, 16)
        b, t, c = x.shape
        h = head_dirs.shape[0]
        hd = c // h
        q3 = (x @ wq).reshape(b, t, h, 3).transpose(0, 2, 1, 3)
        k3 = (x @ wk).reshape(b, t, h, 3).transpose(0, 2, 1, 3)
        v = (x @ wv).reshape(b, t, h, hd).transpose(0, 2, 1, 3)
        q_on_dir = jnp.einsum('bhtd,hd->bht', q3, head_dirs)
        k_on_dir = jnp.einsum('bhtd,hd->bht', k3, head_dirs)
        dot_scores = jnp.einsum('bhtd,bhsd->bhts', q3, k3) * scale
        geo_bias = q_on_dir[..., :, None] * k_on_dir[..., None, :]
        scores = dot_scores + geo_bias
        causal = jnp.tril(jnp.ones((t, t), dtype=bool))
        scores = jnp.where(causal, scores, -jnp.inf)
        attn = jax.nn.softmax(scores, axis=-1)
        out = jnp.einsum('bhts,bhsd->bhtd', attn, v)
        out = out.transpose(0, 2, 1, 3).reshape(b, t, c)
        return out @ wo

    def _L0_ffn_ref(x, Wfc_s, bfc_s, Wproj_s, bproj_s, Wr, Wfc, bfc, Wproj, bproj):
        import jax, jax.numpy as jnp
        import numpy as np
        import math
        N_EMBD = 128
        HIDDEN = 4 * N_EMBD
        N_EXPERTS = 8
        TOP_K = 2
        B, T = (4, 256)

        def new_gelu(x):
            c = math.sqrt(2.0 / math.pi)
            return 0.5 * x * (1.0 + jnp.tanh(c * (x + 0.044715 * x * x * x)))

        def _moe_forward(x, Wfc_s, bfc_s, Wproj_s, bproj_s, Wr, Wfc, bfc, Wproj, bproj):
            Bb, Tt, C = x.shape
            xf = x.reshape(Bb * Tt, C)
            N = Bb * Tt
            shared = new_gelu(xf @ Wfc_s + bfc_s) @ Wproj_s + bproj_s
            logits = xf @ Wr
            probs = jax.nn.softmax(logits, axis=-1)
            topk_p, topk_i = jax.lax.top_k(probs, TOP_K)
            topk_p = topk_p / jnp.sum(topk_p, axis=-1, keepdims=True)
            gate = jnp.zeros((N, N_EXPERTS), dtype=xf.dtype)
            gate = gate.at[jnp.arange(N)[:, None], topk_i].add(topk_p)
            routed = jnp.zeros_like(xf)
            for e in range(N_EXPERTS):
                h = new_gelu(xf @ Wfc[e] + bfc[e]) @ Wproj[e] + bproj[e]
                routed = routed + h * gate[:, e:e + 1]
            return (shared + routed).reshape(Bb, Tt, C)
        return _moe_forward(x, Wfc_s, bfc_s, Wproj_s, bproj_s, Wr, Wfc, bfc, Wproj, bproj)
    x = L0_attn_x
    x = x + _L0_attn_ref(_layernorm(x, axis=-1), L0_attn_wq, L0_attn_wk, L0_attn_wv, L0_attn_wo, L0_attn_head_dirs, L0_attn_scale)
    x = x + _L0_ffn_ref(_layernorm(x, axis=-1), L0_ffn_Wfc_s, L0_ffn_bfc_s, L0_ffn_Wproj_s, L0_ffn_bproj_s, L0_ffn_Wr, L0_ffn_Wfc, L0_ffn_bfc, L0_ffn_Wproj, L0_ffn_bproj)
    return x

_drawn_inputs = setup_inputs


def setup_inputs(seed=0):
    import zlib

    import numpy as np

    out = dict(_drawn_inputs(seed))
    spreads = {'L0_ffn_bfc_s': (0.0, 0.32),
     'L0_ffn_bproj_s': (0.0, 0.1),
     'L0_ffn_bfc': (0.0, 0.506),
     'L0_ffn_bproj': (0.0, 0.1)}
    factors = {}
    for name, (base, spread) in spreads.items():
        noise = np.random.default_rng([zlib.crc32(name.encode()), seed]).standard_normal(out[name].shape)
        drawn = base * np.exp(spread * noise) if base else spread * noise
        out[name] = jnp.asarray(drawn.astype(out[name].dtype))
    for name, factor in factors.items():
        out[name] = (out[name] * factor).astype(out[name].dtype)
    return out
```

```python
from contextlib import ExitStack

import concourse.bass as bass
from concourse import mybir

F32 = mybir.dt.float32
F32R = mybir.dt.float32r
BF16 = mybir.dt.bfloat16
U32 = mybir.dt.uint32
ALU = mybir.AluOpType
ACT = mybir.ActivationFunctionType
AX = mybir.AxisListType

P = 128
B, T, C = 8, 512, 128
H, HD, QD = 16, 8, 3
NT = T // P
R = 4
G = H // R
W = P // R
NE = 8
HID = 512
NQ = HID // P
EPS = 1e-5
NEG = -1e30

NPART = 3
SLOT0 = NPART

UNITS = [(4, (0, 1)), (4, (2, 3)), (3, (0, 1)), (3, (2, 3)), (2, (0, 1, 2, 3)), (1, (0, 1, 2, 3))]
NU = len(UNITS)
PCOL = {4: 0, 3: 512, 2: 896, 1: 1152}
PW = 1280

M_PER, E_PER, Y_PER, GELU_PER = G * NU, G * NU, NE + 1, (NE + 1) * NQ
QKV_STEP, PREP_T1_STEP, STACK_STEP, GT_STEP = 4, 3, 7, 5


def ring_order(prepare):
    order = [("M", k) for k in range(NU)]
    for g in range(G):
        for k in range(NU):
            order += interleave_step(g, k)
    order += [("TO", 0), ("T2", 0)]
    for e in range(NE + 1):
        order += [("H", 2 * e), ("H", 2 * e + 1)]
        if prepare and e == PREP_T1_STEP:
            order.append(("T1", 0))
        if prepare and e == QKV_STEP:
            order.append(("QKV", 0))
        if prepare and e == STACK_STEP:
            order += [("TK", 0), ("TQ", 0)]
    return order


def interleave_step(g, k):
    out = []
    if g + 1 < G:
        ahead = {0: (0, 1), NU - 1: ()}.get(k, (k + 1,))
        out += [("M", NU * (g + 1) + a) for a in ahead]
    return out + [("E", NU * g + k)]


def attn_moe_kernel(nc, x, wq, wk, wv, wo, dirs, scale, wfc_s, bfc_s, wproj_s, bproj_s, wr, wfc, bfc,
                    wproj, bproj, out):
    with ExitStack() as ctx:
        def sb(name, shape, dt=F32):
            return ctx.enter_context(nc.sbuf_tensor(name, shape, dt))

        def sem(name):
            return ctx.enter_context(nc.semaphore(name))

        ident = sb("ident", [P, P])
        identb = sb("identb", [P, P], BF16)
        future = sb("future", [P, P], BF16)
        iota = sb("iota", [P, NE])
        wqkv = sb("wqkv", [P, 2 * H * QD + C])
        dirs_all = sb("dirs_all", [P, H * QD])
        scale_all = sb("scale_all", [P, 1])
        fold = sb("fold", [P, H * QD])
        dots = sb("dots", [P, H])
        wo_sb = sb("wo_sb", [P, C])
        wr_sb = sb("wr_sb", [P, NE])
        w1 = sb("w1", [P, NE + 1, HID])
        w1h = sb("w1h", [P, NE + 1, HID], F32R)
        w1l = sb("w1l", [P, NE + 1, HID], F32R)
        w2 = sb("w2", [P, NE + 1, NQ, C])
        b1rows = sb("b1rows", [(NE + 1) * NQ, P])
        b1 = sb("b1", [P, (NE + 1) * NQ])
        b2 = sb("b2", [NE + 1, C])
        xin = sb("xin", [P, NT, C])
        stats = sb("stats", [P, NT, 6])
        meanvar = sb("meanvar", [P, NT, 2])
        rstd = sb("rstd", [P, NT])
        var_eps = sb("var_eps", [P, NT])
        half = sb("half", [P, NT])
        xn = sb("xn", [P, NT, C])
        xnT = sb("xnT", [P, T])
        parts = sb("parts", [P, NPART, 2, NT, H * QD], BF16)
        rest = sb("rest", [P, 2, NT, H * QD])
        qrows = sb("qrows", [P, NT, H, W], BF16)
        krows = sb("krows", [P, NT, H, W], BF16)
        kst = sb("kst", [P, G, T], BF16)
        qst = sb("qst", [P, G, T], BF16)
        qmst = sb("qmst", [P, 2, T], BF16)
        kpad = sb("kpad", [P, G, R, T], BF16)
        vext = sb("vext", [P, NT, H, W])
        negmax = sb("negmax", [P, G, NT, R])
        mrest = sb("mrest", [P, NT, R])
        probs = sb("probs", [P, 2, R, PW])
        ot = sb("ot", [P, T])
        rsum = sb("rsum", [P, NT, R])
        onorm = sb("onorm", [P, NT, C])
        onT = sb("onT", [P, T])
        x1 = sb("x1", [P, NT, C])
        x2n = sb("x2n", [P, NT, C])
        x2T = sb("x2T", [P, T])
        x2h = sb("x2h", [P, T], F32R)
        x2l = sb("x2l", [P, T], F32R)
        lneg = sb("lneg", [P, NT])
        lsh = sb("lsh", [P, NT, NE])
        pexp = sb("pexp", [P, NT, NE])
        psum_r = sb("psum_r", [P, NT])
        prcp = sb("prcp", [P, NT])
        pr = sb("pr", [P, NT, NE])
        top = sb("top", [P, NT, 8])
        topi = sb("topi", [P, NT, 8], U32)
        topf = sb("topf", [P, NT, 2])
        wsum = sb("wsum", [P, NT])
        wrcp = sb("wrcp", [P, NT])
        wtop = sb("wtop", [P, NT, 2])
        hot = sb("hot", [P, 2, NT, NE])
        gate = sb("gate", [P, NT, NE + 1])
        gateT = sb("gateT", [NE + 1, T])
        hidden = sb("hidden", [P, 2, NQ, T])
        acc = sb("acc", [P, NT, C])
        y = sb("y", [P, NT, C])

        banks = ctx.enter_context(nc.psum_tensor("banks", [P, 8, 512], F32))

        x_loaded, proj_loaded, ffn_loaded = sem("x_loaded"), sem("proj_loaded"), sem("ffn_loaded")
        kpad_loaded, out_stored = sem("kpad_loaded"), sem("out_stored")
        pool_made = sem("pool_made")
        consts_made = sem("consts_made")
        w1_split = sem("w1_split")
        proj_folded = sem("proj_folded")
        b1_turned, b1_ready = sem("b1_turned"), sem("b1_ready")
        var_ready, rstd_ready = sem("var_ready"), sem("rstd_ready")
        dve_step = sem("dve_step")
        ln1_done, xn_turned, xnT_ready = sem("ln1_done"), sem("xn_turned"), sem("xnT_ready")
        qkv_done, v_ready, qkv_free, parts_ready = sem("qkv_done"), sem("v_ready"), sem("qkv_free"), sem("parts_ready")
        k_spread, q_spread = sem("k_spread"), sem("q_spread")
        k_turned, q_turned, kst_ready, qst_ready = sem("k_turned"), sem("q_turned"), sem("kst_ready"), sem("qst_ready")
        m_scores, m_taken, m_parts = sem("m_scores"), sem("m_taken"), sem("m_parts")
        qm_turned, qmst_ready = sem("qm_turned"), sem("qmst_ready")
        scores_ready, exp_done, masked = sem("scores_ready"), sem("exp_done"), sem("masked")
        pv_done, ot_ready, ot_turned, onorm_ready = sem("pv_done"), sem("ot_ready"), sem("ot_turned"), sem("onorm_ready")
        on_turned, onT_ready, proj_done, x1_ready = sem("on_turned"), sem("onT_ready"), sem("proj_done"), sem("x1_ready")
        ln2_done, x2_turned, x2T_ready, x2_split = sem("ln2_done"), sem("x2_turned"), sem("x2T_ready"), sem("x2_split")
        logits_done, logits_taken, pexp_ready = sem("logits_done"), sem("logits_taken"), sem("pexp_ready")
        gates_ready, gate_turned, gateT_ready = sem("gates_ready"), sem("gate_turned"), sem("gateT_ready")
        h_ready, gelu_done, y_done, y_taken, out_ready = sem("h_ready"), sem("gelu_done"), sem("y_done"), sem("y_taken"), sem("out_ready")

        PROJ_LOADS, FFN_LOADS = 6, 8

        def ring(slot):
            return banks[:, 2 * slot:2 * slot + 2, :]

        def flat(slot):
            return ring(slot).rearrange("p a c -> p (a c)")

        PRO = [("T1", 0), ("QKV", 0), ("TK", 0), ("TQ", 0)]
        for prepare in (True, False):
            order = ring_order(prepare)
            assert len(set(order)) == len(order) and (len(order) % 3 == 0 or not prepare)

        def slots(prepare):
            order = PRO + ring_order(prepare)
            return {u: n % 3 for n, u in enumerate(order) if n >= len(PRO)}, {
                u: order[n - 3] if n - 3 >= len(PRO) else None for n, u in enumerate(order) if n >= len(PRO)}

        PRO_SLOT = {u: n % 3 for n, u in enumerate(PRO)}

        def unit_view(slot, tiles):
            if tiles >= 3:
                return ring(slot)[:, :, 0:P * tiles]
            if tiles == 2:
                return flat(slot).rearrange("p (n w) -> p n w", w=2 * P)
            return banks[:, 2 * slot, :].rearrange("p (n w) -> p n w", w=P)

        def opens_bank(tiles, n):
            return tiles >= 3 or (tiles == 2 and n % 2 == 0) or n == 0

        def six(cols=512):
            return banks[:, 6, 0:cols]

        def seven(cols=512):
            return banks[:, 7, 0:cols]

        def y_bank(e):
            return banks[:, 7 - e % 2, :].rearrange("p (i c) -> p i c", i=NT)

        def wait_earlier(eng, semaphore, value):
            if not isinstance(value, int) or value > 0:
                eng.wait_ge(semaphore, value)

        def wait_apart(eng, semaphore, value):
            eng.wait_ge(consts_made, 1)
            eng.wait_ge(semaphore, value)

        def batch_loop(eng, body):
            body(0, True)
            with eng.Fori(1, B - 1) as b:
                body(b, True)
            body(B - 1, False)

        block = ctx.enter_context(nc.Block())

        @block.sync
        def _(sp):
            xv = x.rearrange("b (i p) c -> p (b i) c", p=P)
            ov = out.rearrange("b (i p) c -> p (b i) c", p=P)
            sp.dma_start(xin[:], xv[:, 0:NT, :]).then_inc(x_loaded, 16)
            sp.dma_start(wqkv[:, 0:48], wq).then_inc(proj_loaded, 16)
            sp.dma_start(wqkv[:, 48:96], wk).then_inc(proj_loaded, 16)
            sp.dma_start(wqkv[:, 96:224], wv).then_inc(proj_loaded, 16)
            sp.dma_start(dirs_all[:], dirs.rearrange("(o h) d -> o (h d)", o=1).partition_broadcast(P)).then_inc(proj_loaded, 16)
            sp.dma_start(scale_all[:], scale.rearrange("(o h) -> o h", o=1).partition_broadcast(P)).then_inc(proj_loaded, 16)
            sp.dma_start(wo_sb[:], wo).then_inc(proj_loaded, 16)
            sp.dma_start(w1[:, 0:NE, :], wfc.rearrange("e c h -> c e h")).then_inc(ffn_loaded, 16)
            sp.dma_start(w1[:, NE, :], wfc_s).then_inc(ffn_loaded, 16)
            sp.dma_start(w2[:, 0:NE].rearrange("p e q n -> p (e q) n"), wproj.rearrange("e (q p) n -> p (e q) n", p=P)).then_inc(ffn_loaded, 16)
            sp.dma_start(w2[:, NE], wproj_s.rearrange("(q p) n -> p q n", p=P)).then_inc(ffn_loaded, 16)
            sp.dma_start(b1rows[0:NE * NQ, :], bfc.rearrange("e (q p) -> (e q) p", p=P)).then_inc(ffn_loaded, 16)
            sp.dma_start(b1rows[NE * NQ:(NE + 1) * NQ, :], bfc_s.rearrange("(q p) -> q p", p=P)).then_inc(ffn_loaded, 16)
            sp.dma_start(b2[0:NE, :], bproj).then_inc(ffn_loaded, 16)
            sp.dma_start(b2[NE:NE + 1, :], bproj_s.rearrange("(o n) -> o n", o=1)).then_inc(ffn_loaded, 16)
            sp.dma_start(wr_sb[:], wr).then_inc(ffn_loaded, 16)

            def spread_k(bb):
                wait_apart(sp, kst_ready, bb + 1)
                for r in range(R):
                    sp.dma_start(kpad[W * r:W * r + W, :, r, :], kst[W * r:W * r + W, :, :]).then_inc(kpad_loaded, 16)

            def body(b, prepare):
                if prepare:
                    wait_apart(sp, x1_ready, b + 1)
                    sp.dma_start(xin[:], xv[:, bass.ds(b * NT + NT, NT), :]).then_inc(x_loaded, 16)
                    spread_k(b + 1)
                wait_apart(sp, out_ready, b + 1)
                sp.dma_start(ov[:, bass.ds(b * NT, NT), :], y[:]).then_inc(out_stored, 16)

            sp.wait_ge(consts_made, 1)
            spread_k(0)
            batch_loop(sp, body)
            sp.wait_ge(out_stored, 16 * B)

        @block.gpsimd
        def _(pool):
            made = 0
            unit_seen = pool.alloc_register("unit_seen")
            batch_seen = pool.alloc_register("batch_seen")
            group_seen = pool.alloc_register("group_seen")
            batch_next = pool.alloc_register("batch_next")
            for counter in (unit_seen, batch_seen, group_seen):
                pool.reg_mov(counter, 0)
            pool.reg_mov(batch_next, 1)

            def link(ins):
                nonlocal made
                made += 1
                ins.then_inc(pool_made, 1)
                pool.wait_ge(pool_made, made)

            def root(nth):
                pool.wait_ge(var_ready, nth)
                pool.tensor_tensor(rstd[:], var_eps[:], half[:], ALU.pow).then_inc(rstd_ready, 1)

            pool.memset(ident[:], 0.0)
            pool.memset(identb[:], 0.0)
            pool.memset(future[:], 0.0)
            pool.memset(qrows[:], 0.0)
            pool.memset(krows[:], 0.0)
            link(pool.memset(vext[:], 0.0))
            for m in (ident, identb):
                pool.affine_select(out=m[:], in_=m[:], compare_op=ALU.not_equal, fill=1.0, base=0,
                                   pattern=[[-1, P]], channel_multiplier=1)
            pool.affine_select(out=future[:], in_=future[:], compare_op=ALU.is_ge, fill=NEG, base=0,
                               pattern=[[-1, P]], channel_multiplier=1)
            pool.memset(vext[:, :, :, HD:HD + 1], 1.0)
            pool.memset(gate[:], 1.0)
            link(pool.memset(half[:], -0.5))
            root(1)
            pool.memset(krows[:, :, :, 0:NPART], 1.0)
            pool.memset(kpad[:].rearrange("p g r t -> p (g r t)").bitcast(F32), 0.0).then_inc(consts_made, 1)

            def spread_parts(first=False):
                if first:
                    pool.wait_ge(parts_ready, 1)
                else:
                    pool.reg_add(batch_seen, batch_seen, 1)
                    pool.reg_add(batch_next, batch_next, 1)
                    pool.reg_add(group_seen, group_seen, G)
                    pool.wait_ge(consts_made, 1)
                    pool.wait_ge(parts_ready, batch_next)
                    pool.wait_ge(k_turned, batch_seen)
                qv = qrows[:].rearrange("p i h s -> p (i h) s")
                kv = krows[:].rearrange("p i h s -> p (i h) s")

                def part(n, which):
                    v = parts[:, n, which].rearrange("p i (h d) -> p (i h) d", d=QD)
                    return v.unsqueeze(2).to_broadcast([P, NT * H, NPART, QD])

                for c in range(NPART):
                    dst = kv[:, :, SLOT0:SLOT0 + 27].rearrange("p h (a c d) -> p h a c d", a=NPART, c=NPART)[:, :, :, c, :]
                    last = pool.tensor_copy(dst, part(c, 1))
                last.then_inc(k_spread, 1)
                if not first:
                    pool.wait_ge(consts_made, 1)
                    pool.wait_ge(qm_turned, group_seen)
                pool.memset(qv[:, :, 0:NPART], 0.0)
                for a in range(NPART):
                    dst = qv[:, :, SLOT0 + 9 * a:SLOT0 + 9 * a + 9].rearrange("p h (c d) -> p h c d", c=NPART)
                    last = pool.tensor_copy(dst, part(a, 0))
                last.then_inc(q_spread, 1)

            def mask_probs(b, g):
                for k, (tiles, heads) in enumerate(UNITS):
                    pool.reg_add(unit_seen, unit_seen, 1)
                    pool.wait_ge(consts_made, 1)
                    pool.wait_ge(exp_done, unit_seen)
                    v = probs[:, g % 2, heads[0]:heads[-1] + 1, PCOL[tiles]:PCOL[tiles] + P]
                    pool.affine_select(out=v, in_=v, compare_op=ALU.is_ge, fill=0.0, base=0,
                                       pattern=[[0, len(heads)], [1, P]], channel_multiplier=-1).then_inc(masked, 1)

            def body(b, prepare):
                for g in range(G):
                    mask_probs(b, g)
                root(2 * b + 2)
                if prepare:
                    root(2 * b + 3)
                    spread_parts()

            spread_parts(first=True)
            pool.wait_ge(ffn_loaded, 16 * 9)
            for e in range(NE + 1):
                pool.tensor_copy(w1h[:, e, :], w1[:, e, :]).then_inc(pool_made, 1)
                made += 1
            for e in range(NE + 1):
                pool.wait_ge(pool_made, made - NE + e)
                pool.tensor_tensor(w1l[:, e, :], w1[:, e, :], w1h[:, e, :].bitcast(F32), ALU.subtract).then_inc(w1_split, 1)
            batch_loop(pool, body)

        @block.scalar
        def _(act):
            def copy(dst, src):
                return nc.scalar.activation(dst, src, ACT.Copy)

            def evacuate_xn(bb, slot):
                act.wait_ge(xn_turned, bb + 1)
                wait_earlier(act, qkv_done, bb)
                copy(xnT[:], flat(slot)[:, 0:T]).then_inc(xnT_ready, 1)

            def evacuate_v(bb, slot):
                act.wait_ge(qkv_done, bb + 1)
                wait_earlier(act, pv_done, bb * G)
                src = flat(slot).rearrange("p (i c) -> p i c", i=NT)[:, :, 96:224]
                copy(vext[:, :, :, 0:HD], src.rearrange("p i (h d) -> p i h d", d=HD)).then_inc(v_ready, 1)

            def evacuate_stacks(bb, kslot, qslot):
                act.wait_ge(k_turned, bb + 1)
                wait_earlier(act, kpad_loaded, bb * 16 * R)
                copy(kst[:].rearrange("p g t -> p (g t)"), flat(kslot).bitcast(BF16)).then_inc(kst_ready, 1)
                act.wait_ge(q_turned, bb + 1)
                wait_earlier(act, m_scores, bb * M_PER)
                copy(qst[:].rearrange("p g t -> p (g t)"), flat(qslot).bitcast(BF16)).then_inc(qst_ready, 1)

            act.wait_ge(consts_made, 1)
            evacuate_xn(0, PRO_SLOT["T1", 0])
            evacuate_v(0, PRO_SLOT["QKV", 0])
            evacuate_stacks(0, PRO_SLOT["TK", 0], PRO_SLOT["TQ", 0])

            def exps(b, g, slot):
                for k, (tiles, heads) in enumerate(UNITS):
                    act.wait_ge(scores_ready, b * E_PER + g * NU + k + 1)
                    wait_earlier(act, pv_done, b * G + max(0, g - 1))
                    nc.scalar.activation(probs[:, g % 2, heads[0]:heads[-1] + 1, PCOL[tiles]:PCOL[tiles] + P * tiles],
                                         unit_view(slot["E", g * NU + k], tiles), ACT.Exp).then_inc(exp_done, 1)

            def evacuate_o(b, g):
                act.wait_ge(pv_done, b * G + g + 1)
                wait_earlier(act, ot_turned, b * G + g)
                copy(ot[:], six()).then_inc(ot_ready, 1)

            def body(b, prepare):
                slot, _ = slots(prepare)
                for g in range(G):
                    exps(b, g, slot)
                    if g >= 1:
                        evacuate_o(b, g - 1)
                evacuate_o(b, G - 1)
                act.wait_ge(on_turned, b + 1)
                copy(onT[:], flat(slot["TO", 0])[:, 0:T]).then_inc(onT_ready, 1)
                act.wait_ge(x2_turned, b + 1)
                copy(x2T[:], flat(slot["T2", 0])[:, 0:T]).then_inc(x2T_ready, 1)
                act.wait_ge(logits_taken, b + 1)
                nc.scalar.activation(pexp[:], lsh[:], ACT.Exp).then_inc(pexp_ready, 1)
                for e in range(NE + 1):
                    for q in range(NQ):
                        if q % 2 == 0:
                            act.wait_ge(h_ready, b * 2 * (NE + 1) + 2 * e + q // 2 + 1)
                        if q == 0:
                            wait_earlier(act, y_done, b * Y_PER + max(0, e - 1))
                        nc.scalar.activation(hidden[:, e % 2, q, :], ring(slot["H", 2 * e + q // 2])[:, q % 2, :],
                                             ACT.Gelu_apprx_tanh, bias=b1[:, e * NQ + q:e * NQ + q + 1]).then_inc(gelu_done, 1)
                    if prepare and e == PREP_T1_STEP:
                        evacuate_xn(b + 1, slot["T1", 0])
                    if prepare and e == QKV_STEP:
                        evacuate_v(b + 1, slot["QKV", 0])
                    if prepare and e == STACK_STEP:
                        evacuate_stacks(b + 1, slot["TK", 0], slot["TQ", 0])
                    if e == GT_STEP:
                        act.wait_ge(gate_turned, b + 1)
                        copy(gateT[:], six()[0:NE + 1, :]).then_inc(gateT_ready, 1)

            act.wait_ge(b1_ready, 1)
            batch_loop(act, body)

        @block.vector
        def _(dve):
            class Chain:

                def __init__(self):
                    dve.sem_clear(dve_step)
                    self.n = 0

                def __call__(self, ins):
                    self.n += 1
                    ins.then_inc(dve_step, 1)
                    dve.wait_ge(dve_step, self.n)

            def bc(ap, n):
                shape = list(ap.shape) + [n]
                return ap.unsqueeze(len(ap.shape)).to_broadcast(shape)

            def layernorm(link, dst, src, nth):
                for i in range(NT):
                    last = dve.bn_stats(stats[:, i, :], src[:, i, :])
                link(last)
                for i in range(NT):
                    last = dve.bn_aggr(meanvar[:, i, :], stats[:, i, :])
                link(last)
                dve.tensor_scalar(var_eps[:], meanvar[:, :, 1], EPS, None, ALU.add).then_inc(var_ready, 1)
                dve.wait_ge(rstd_ready, nth)
                for i in range(NT):
                    last = dve.tensor_scalar(dst[:, i, :], src[:, i, :], meanvar[:, i, 0:1], rstd[:, i:i + 1],
                                             ALU.subtract, ALU.mult)
                return last

            def first_norm(bb, link):
                dve.wait_ge(x_loaded, bb * 16 + 16)
                wait_earlier(dve, xn_turned, bb)
                layernorm(link, xn, xin, 2 * bb + 1).then_inc(ln1_done, 1)

            def split_qk(bb, link, slot):
                dve.wait_ge(v_ready, bb + 1)
                wait_earlier(dve, q_spread, bb)
                qk = flat(slot).rearrange("p (i c) -> p i c", i=NT)[:, :, 0:96].rearrange("p i (w c) -> p w i c", w=2)
                link(dve.tensor_copy(parts[:, 0], qk))
                dve.tensor_tensor(rest[:], qk, parts[:, 0], ALU.subtract).then_inc(qkv_free, 1)
                dve.wait_ge(qkv_free, bb + 1)
                link(dve.tensor_copy(parts[:, 1], rest[:]))
                dve.tensor_tensor(parts[:, 2], rest[:], parts[:, 1], ALU.subtract).then_inc(parts_ready, 1)

            def take_maxima(b, g, slot):
                for k, (tiles, heads) in enumerate(UNITS):
                    dve.wait_ge(m_scores, b * M_PER + g * NU + k + 1)
                    dve.tensor_reduce(negmax[:, g, tiles - 1, heads[0]:heads[-1] + 1], unit_view(slot["M", g * NU + k], tiles),
                                      AX.X, ALU.max, negate=True).then_inc(m_taken, 1)

            def split_maxima(b, g, link):
                dve.wait_ge(m_taken, b * M_PER + g * NU + NU)
                dst = qrows[:, :, R * g:R * g + R, :]
                link(dve.tensor_copy(dst[:, :, :, 0], negmax[:, g]))
                link(dve.tensor_tensor(mrest[:], negmax[:, g], dst[:, :, :, 0], ALU.subtract))
                link(dve.tensor_copy(dst[:, :, :, 1], mrest[:]))
                dve.tensor_tensor(dst[:, :, :, 2], mrest[:], dst[:, :, :, 1], ALU.subtract).then_inc(m_parts, 1)

            def evacuate_qm(b, g):
                dve.wait_ge(qm_turned, b * G + g + 1)
                wait_earlier(dve, scores_ready, b * E_PER + NU * max(0, g - 1))
                dve.tensor_copy(qmst[:, g % 2, :], seven(256).bitcast(BF16)).then_inc(qmst_ready, 1)

            def normalize(b, g, link):
                dve.wait_ge(ot_turned, b * G + g + 1)
                src = seven().rearrange("p (i r w) -> p i r w", i=NT, r=R)
                link(dve.reciprocal(rsum[:], src[:, :, :, HD]))
                dst = onorm[:].rearrange("p i (g r d) -> p i g r d", g=G, r=R)[:, :, g]
                dve.tensor_tensor(dst, src[:, :, :, 0:HD], bc(rsum[:], HD), ALU.mult).then_inc(onorm_ready, 1)

            def route(b, link):
                dve.wait_ge(logits_done, b + 1)
                logits = six(NT * NE).rearrange("p (i e) -> p i e", i=NT)
                link(dve.tensor_reduce(lneg[:], logits, AX.X, ALU.max, negate=True))
                dve.tensor_tensor(lsh[:], logits, bc(lneg[:], NE), ALU.add).then_inc(logits_taken, 1)
                dve.wait_ge(pexp_ready, b + 1)
                link(dve.tensor_reduce(psum_r[:], pexp[:], AX.X, ALU.add))
                link(dve.reciprocal(prcp[:], psum_r[:]))
                link(dve.tensor_tensor(pr[:], pexp[:], bc(prcp[:], NE), ALU.mult))
                for i in range(NT):
                    last = dve.max(top[:, i, :], pr[:, i, :])
                link(last)
                for i in range(NT):
                    last = dve.max_index(topi[:, i, :], top[:, i, :], pr[:, i, :])
                dve.tensor_tensor(wsum[:], top[:, :, 0], top[:, :, 1], ALU.add)
                link(last)
                link(dve.tensor_copy(topf[:], topi[:, :, 0:2]))
                link(dve.reciprocal(wrcp[:], wsum[:]))
                link(dve.tensor_tensor(wtop[:], top[:, :, 0:2], bc(wrcp[:], 2), ALU.mult))
                every = iota[:].unsqueeze(1).to_broadcast([P, NT, NE])
                for n in range(2):
                    last = dve.tensor_tensor(hot[:, n], every, bc(topf[:, :, n], NE), ALU.is_equal)
                link(last)
                for n in range(2):
                    last = dve.tensor_tensor(hot[:, n], hot[:, n], bc(wtop[:, :, n], NE), ALU.mult)
                link(last)
                dve.tensor_tensor(gate[:, :, 0:NE], hot[:, 0], hot[:, 1], ALU.add).then_inc(gates_ready, 1)

            def add_expert(b, e):
                dve.wait_ge(y_done, b * Y_PER + e + 1)
                src = y_bank(e)
                if e == NE:
                    dve.wait_ge(y_taken, b * NE + e)
                    wait_earlier(dve, out_stored, b * 16)
                    dve.tensor_tensor(y[:], src, acc[:], ALU.add).then_inc(out_ready, 1)
                    return
                dve.wait_ge(gates_ready, b + 1)
                if e > 0:
                    dve.wait_ge(y_taken, b * NE + e)
                for i in range(NT):
                    last = dve.scalar_tensor_tensor(acc[:, i, :], src[:, i, :], gate[:, i, e:e + 1],
                                                    (acc if e else x1)[:, i, :], ALU.mult, ALU.add)
                last.then_inc(y_taken, 1)

            def body(b, prepare):
                slot, _ = slots(prepare)
                link = Chain()
                for g in range(G):
                    take_maxima(b, g, slot)
                    split_maxima(b, g, link)
                    evacuate_qm(b, g)
                    if g >= 2:
                        normalize(b, g - 2, link)
                normalize(b, G - 2, link)
                normalize(b, G - 1, link)
                dve.wait_ge(proj_done, b + 1)
                dve.tensor_tensor(x1[:], banks[:, 7, :].rearrange("p (i c) -> p i c", i=NT), xin[:], ALU.add).then_inc(x1_ready, 1)
                dve.wait_ge(x1_ready, b + 1)
                layernorm(link, x2n, x1, 2 * b + 2).then_inc(ln2_done, 1)
                dve.wait_ge(x2T_ready, b + 1)
                link(dve.tensor_copy(x2h[:], x2T[:]))
                dve.tensor_tensor(x2l[:], x2T[:], x2h[:].bitcast(F32), ALU.subtract).then_inc(x2_split, 1)
                route(b, link)
                for e in range(NE + 1):
                    add_expert(b, e)
                    if prepare and e == 0:
                        first_norm(b + 1, link)
                    if prepare and e == QKV_STEP - 1:
                        split_qk(b + 1, link, slot["QKV", 0])

            link = Chain()
            first_norm(0, link)
            dve.wait_ge(proj_loaded, 16 * PROJ_LOADS)
            wk3 = wqkv[:, 48:96]
            link(dve.tensor_tensor(fold[:], wk3, dirs_all[:], ALU.mult))
            link(dve.tensor_reduce(dots[:], fold[:].rearrange("p (h d) -> p h d", d=QD), AX.X, ALU.add))
            link(dve.tensor_tensor(fold[:].rearrange("p (h d) -> p h d", d=QD), dirs_all[:].rearrange("p (h d) -> p h d", d=QD),
                                   bc(dots[:], QD), ALU.mult))
            dve.scalar_tensor_tensor(wk3, wk3, scale_all[:, 0:1], fold[:], ALU.mult, ALU.add).then_inc(proj_folded, 1)
            for e in range(NE):
                dve.memset(iota[:, e:e + 1], float(e))
            split_qk(0, link, PRO_SLOT["QKV", 0])
            dve.wait_ge(b1_turned, 1)
            dve.tensor_copy(b1[:], banks[:, 6, 0:(NE + 1) * NQ]).then_inc(b1_ready, 1)
            dve.wait_ge(b1_ready, 1)
            batch_loop(dve, body)

        @block.tensor
        def _(pe):
            mm = nc.tensor.matmul

            def turn(dst, src, eye):
                return nc.tensor.transpose(dst, src, eye)

            def turn_xn(bb, slot):
                pe.wait_ge(ln1_done, bb + 1)
                for i in range(NT):
                    last = turn(flat(slot)[:, P * i:P * i + P], xn[:, i, :], ident[:])
                last.then_inc(xn_turned, 1)

            def project(bb, slot):
                pe.wait_ge(xnT_ready, bb + 1)
                for i in range(NT):
                    last = mm(flat(slot)[:, 2 * P * i:2 * P * i + 224], xnT[:, P * i:P * i + P], wqkv[:], start=True, stop=True)
                last.then_inc(qkv_done, 1)

            def turn_stacks(bb, slot, rows, spread, turned):
                pe.wait_ge(spread, bb + 1)
                dst = flat(slot).bitcast(BF16)
                for g in range(G):
                    for i in range(NT):
                        last = turn(dst[:, T * g + P * i:T * g + P * i + P],
                                    rows[:, i, R * g:R * g + R, :].rearrange("p h s -> p (h s)"), identb[:])
                last.then_inc(turned, 1)

            def body(b, prepare):
                slot, before = slots(prepare)

                def free(unit):
                    kind, k = before[unit] or ("H", -1)
                    if kind == "M":
                        pe.wait_ge(m_taken, b * M_PER + k + 1)
                    elif kind == "E":
                        pe.wait_ge(exp_done, b * E_PER + k + 1)
                    elif kind == "H":
                        wait_earlier(pe, gelu_done, b * GELU_PER + 2 * (k + 1))
                    elif kind == "TO":
                        pe.wait_ge(onT_ready, b + 1)
                    elif kind == "T2":
                        pe.wait_ge(x2T_ready, b + 1)
                    elif kind == "T1":
                        pe.wait_ge(xnT_ready, b + 2)
                    elif kind == "QKV":
                        pe.wait_ge(qkv_free, b + 2)
                    elif kind == "TK":
                        pe.wait_ge(kst_ready, b + 2)
                    elif kind == "TQ":
                        pe.wait_ge(qst_ready, b + 2)

                def max_scores(n):
                    g, (tiles, heads) = n // NU, UNITS[n % NU]
                    free(("M", n))
                    dst, i = unit_view(slot["M", n], tiles), tiles - 1
                    for m, r in enumerate(heads):
                        mm(dst[:, m, :], qst[:, g, P * i:P * i + P], kpad[:, g, r, 0:P * tiles],
                           start=opens_bank(tiles, m), stop=False, skip_group_check=True)
                        last = mm(dst[:, m, P * i:P * i + P], identb[:], future[:], start=False, stop=True,
                                  skip_group_check=True)
                    last.then_inc(m_scores, 1)

                def scores(n):
                    g, (tiles, heads) = n // NU, UNITS[n % NU]
                    free(("E", n))
                    if n % NU == 0:
                        pe.wait_ge(qmst_ready, b * G + g + 1)
                    dst, j = unit_view(slot["E", n], tiles), NT - tiles
                    for m, r in enumerate(heads):
                        last = mm(dst[:, m, :], kpad[:, g, r, P * j:P * j + P], qmst[:, g % 2, P * j:T],
                                  start=opens_bank(tiles, m), stop=True, skip_group_check=True)
                    last.then_inc(scores_ready, 1)

                def turn_maxima(g):
                    pe.wait_ge(m_parts, b * G + g + 1)
                    if g == 0:
                        wait_earlier(pe, out_ready, b)
                    elif g < G - 1:
                        pe.wait_ge(qmst_ready, b * G + g)
                    else:
                        pe.wait_ge(onorm_ready, b * G + 1)
                    dst = seven(256).bitcast(BF16)
                    for i in range(NT):
                        last = turn(dst[:, P * i:P * i + P], qrows[:, i, R * g:R * g + R, :].rearrange("p h s -> p (h s)"),
                                    identb[:])
                    last.then_inc(qm_turned, 1)

                def values(g):
                    pe.wait_ge(masked, b * E_PER + g * NU + NU)
                    if g == 0:
                        pe.wait_ge(v_ready, b + 1)
                        wait_earlier(pe, y_taken, b * NE)
                    else:
                        pe.wait_ge(ot_ready, b * G + g)
                    for j in range(NT):
                        tiles = NT - j
                        for r in range(R):
                            last = mm(banks[W * r:W * r + W, 6, P * j:T], vext[:, j, R * g + r, :],
                                      probs[:, g % 2, r, PCOL[tiles]:PCOL[tiles] + P * tiles], start=(j == 0), stop=(j == NT - 1))
                    last.then_inc(pv_done, 1)

                def turn_values(g):
                    pe.wait_ge(ot_ready, b * G + g + 1)
                    if g < 2:
                        pe.wait_ge(qmst_ready, b * G + g + 3)
                    else:
                        pe.wait_ge(onorm_ready, b * G + g)
                    for i in range(NT):
                        last = turn(seven()[:, P * i:P * i + P], ot[:, P * i:P * i + P], ident[:])
                    last.then_inc(ot_turned, 1)

                def first_layer(e, u):
                    free(("H", 2 * e + u))
                    for q in (2 * u, 2 * u + 1):
                        dst = ring(slot["H", 2 * e + u])[:, q % 2, :]
                        wh, wl = w1h[:, e, P * q:P * q + P], w1l[:, e, P * q:P * q + P]
                        mm(dst, wh, x2h[:], start=True, stop=False)
                        mm(dst, wh, x2l[:], start=False, stop=False)
                        last = mm(dst, wl, x2h[:], start=False, stop=True)
                    last.then_inc(h_ready, 1)

                def second_layer(e):
                    pe.wait_ge(gelu_done, b * GELU_PER + NQ * e + NQ)
                    if e == 0:
                        pe.wait_ge(x1_ready, b + 1)
                    elif e == 1:
                        pe.wait_ge(logits_taken, b + 1)
                    elif e == GT_STEP:
                        pe.wait_ge(gateT_ready, b + 1)
                    else:
                        pe.wait_ge(y_taken, b * NE + e - 1)
                    for i in range(NT):
                        for q in range(NQ):
                            last = mm(y_bank(e)[:, i, :], hidden[:, e % 2, q, P * i:P * i + P], w2[:, e, q, :],
                                      start=(q == 0), stop=(q == NQ - 1 and e < NE))
                        if e == NE:
                            last = mm(y_bank(e)[:, i, :], gateT[:, P * i:P * i + P], b2[:], start=False, stop=True)
                    last.then_inc(y_done, 1)

                pe.wait_ge(kpad_loaded, b * 16 * R + 16 * R)
                pe.wait_ge(qst_ready, b + 1)
                for k in range(NU):
                    max_scores(k)
                turn_maxima(0)
                for g in range(G):
                    for k in range(NU):
                        for kind, n in interleave_step(g, k):
                            max_scores(n) if kind == "M" else scores(n)
                    if g >= 1:
                        values(g - 1)
                    if g + 1 < G:
                        turn_maxima(g + 1)
                    if g >= 1:
                        turn_values(g - 1)
                values(G - 1)
                turn_values(G - 1)
                free(("TO", 0))
                pe.wait_ge(onorm_ready, b * G + G)
                for i in range(NT):
                    last = turn(flat(slot["TO", 0])[:, P * i:P * i + P], onorm[:, i, :], ident[:])
                last.then_inc(on_turned, 1)
                pe.wait_ge(onT_ready, b + 1)
                for i in range(NT):
                    last = mm(seven()[:, P * i:P * i + P], onT[:, P * i:P * i + P], wo_sb[:], start=True, stop=True)
                last.then_inc(proj_done, 1)
                free(("T2", 0))
                pe.wait_ge(ln2_done, b + 1)
                for i in range(NT):
                    last = turn(flat(slot["T2", 0])[:, P * i:P * i + P], x2n[:, i, :], ident[:])
                last.then_inc(x2_turned, 1)
                pe.wait_ge(ot_ready, b * G + G)
                pe.wait_ge(x2T_ready, b + 1)
                for i in range(NT):
                    last = mm(six()[:, NE * i:NE * i + NE], x2T[:, P * i:P * i + P], wr_sb[:], start=True, stop=True)
                last.then_inc(logits_done, 1)
                pe.wait_ge(x2_split, b + 1)
                for e in range(NE + 1):
                    first_layer(e, 0)
                    first_layer(e, 1)
                    if prepare and e == PREP_T1_STEP:
                        free(("T1", 0))
                        turn_xn(b + 1, slot["T1", 0])
                    if prepare and e == QKV_STEP:
                        free(("QKV", 0))
                        project(b + 1, slot["QKV", 0])
                    if prepare and e == STACK_STEP:
                        free(("TK", 0))
                        turn_stacks(b + 1, slot["TK", 0], krows, k_spread, k_turned)
                        free(("TQ", 0))
                        turn_stacks(b + 1, slot["TQ", 0], qrows, q_spread, q_turned)
                    if e > 0:
                        second_layer(e - 1)
                    if e == GT_STEP:
                        pe.wait_ge(gates_ready, b + 1)
                        pe.wait_ge(y_taken, b * NE + GT_STEP - 1)
                        for i in range(NT):
                            last = turn(six()[0:NE + 1, P * i:P * i + P], gate[:, i, :], ident[:])
                        last.then_inc(gate_turned, 1)
                second_layer(NE)

            pe.wait_ge(consts_made, 1)
            pe.wait_ge(ffn_loaded, 16 * 9)
            turn(banks[:, 6, 0:(NE + 1) * NQ], b1rows[:], ident[0:(NE + 1) * NQ, 0:(NE + 1) * NQ]).then_inc(b1_turned, 1)
            turn_xn(0, PRO_SLOT["T1", 0])
            pe.wait_ge(proj_folded, 1)
            project(0, PRO_SLOT["QKV", 0])
            turn_stacks(0, PRO_SLOT["TK", 0], krows, k_spread, k_turned)
            turn_stacks(0, PRO_SLOT["TQ", 0], qrows, q_spread, q_turned)
            pe.wait_ge(b1_ready, 1)
            pe.wait_ge(w1_split, NE + 1)
            batch_loop(pe, body)


_INS = ["L0_attn_x", "L0_attn_wq", "L0_attn_wk", "L0_attn_wv", "L0_attn_wo", "L0_attn_head_dirs", "L0_attn_scale",
        "L0_ffn_Wfc_s", "L0_ffn_bfc_s", "L0_ffn_Wproj_s", "L0_ffn_bproj_s", "L0_ffn_Wr", "L0_ffn_Wfc", "L0_ffn_bfc",
        "L0_ffn_Wproj", "L0_ffn_bproj"]


def kernel(**inputs):
    import numpy as _np
    import concourse.bacc as _bacc
    from concourse import mybir as _mybir
    from concourse.bass_utils import run_bass_kernel_spmd as _run

    nc = _bacc.Bacc("TRN2", target_bir_lowering=False, num_devices=1)
    arrays, args = {}, []
    for name in _INS:
        a = _np.ascontiguousarray(inputs[name])
        arrays[f"in_{name}"] = a
        args.append(nc.dram_tensor(f"in_{name}", a.shape, _mybir.dt.from_np(a.dtype), kind="ExternalInput").ap())
    args.append(nc.dram_tensor("out_0", (B, T, C), _mybir.dt.float32, kind="ExternalOutput").ap())
    attn_moe_kernel(nc, *args)
    r = _run(nc, [arrays], core_ids=[0])
    return r.results[0]["out_0"]
```

```python
from contextlib import ExitStack

import concourse.bass as bass
from concourse import mybir

F32 = mybir.dt.float32
F32R = mybir.dt.float32r
BF16 = mybir.dt.bfloat16
U32 = mybir.dt.uint32
ALU = mybir.AluOpType
ACT = mybir.ActivationFunctionType
AX = mybir.AxisListType

P = 128
B, T, C = 8, 512, 128
H, HD, QD = 16, 8, 3
NT = T // P
R = 4
G = H // R
W = P // R
NE = 8
HID = 512
NQ = HID // P
EPS = 1e-5
NEG = -1e30

NPART = 3
SLOT0 = NPART

UNITS = [(4, (0, 1)), (4, (2, 3)), (3, (0, 1)), (3, (2, 3)), (2, (0, 1, 2, 3)), (1, (0, 1, 2, 3))]
NU = len(UNITS)
PCOL = {4: 0, 3: 512, 2: 896, 1: 1152}
PW = 1280

M_PER, E_PER, Y_PER, GELU_PER = G * NU, G * NU, NE + 1, (NE + 1) * NQ

ATTENTION = ("M", "E", "TM", "PV", "TP", "TO", "PJ", "T2", "RL")
EXPERTS = ("H", "Y", "GT")
PREPARATION = ("T1", "QKV", "TK", "TQ")


def hidden_steps(e):
    return [("H", 2 * e), ("H", 2 * e + 1)]


def out_steps(e):
    return [("Y", NT * e + i) for i in range(NT)]


def batch_steps(experts, prepare):
    h = [hidden_steps(e) for e in range(NE + 1)]
    y = [out_steps(e) for e in range(NE + 1)]

    def m(g, *ks):
        return [("M", NU * g + k) for k in ks]

    steps = h[0] + m(0, 0) + h[1] + m(0, 1, 2) + y[0][:1] + m(0, 3) + y[0][1:2] + m(0, 4, 5) + y[0][2:] + m(1, 0, 1)
    steps += [("TM", 0)]
    for g in range(G):
        fill = y[1] if g == 0 else y[2 * g] + y[2 * g + 1]
        take = {0: (0, 1, 1, 1, 1, 0), 3: (1, 1, 1, 1, 1, 1)}.get(g, (1, 2, 1, 1, 2, 1))
        for k in range(NU):
            if g + 1 < G and k + 2 < NU:
                steps += m(g + 1, k + 2)
            steps.append(("E", NU * g + k))
            steps += fill[:take[k]]
            fill = fill[take[k]:]
        if g < G - 1:
            first, second = h[2 * g + 2], h[2 * g + 3]
            steps += first[:1] + [("TM", g + 1)] + first[1:]
            steps += [("PV", g - 1)] if g else [("GT", 0)]
            steps += second + ([("TP", g - 1)] if g else [])
            steps += {0: [("T1", 0)], 1: [("QKV", 0)]}.get(g, [])
            if g + 2 < G:
                steps += m(g + 2, 0, 1)
    steps += [("PV", G - 2)] + fill + [("PV", G - 1)] + h[NE][:1] + [("TP", G - 2)] + h[NE][1:] + [("TP", G - 1)]
    steps += [("TK", 0), ("TO", 0), ("TQ", 0), ("PJ", 0)] + y[NE] + [("T2", 0), ("RL", 0)]
    return [s for s in steps if (experts or s[0] not in EXPERTS) and (prepare or s[0] not in PREPARATION)]


def expert_steps():
    steps = hidden_steps(0)
    for e in range(NE + 1):
        if e < NE:
            steps += hidden_steps(e + 1)
        if e == 2:
            steps.append(("GT", 0))
        steps += out_steps(e)
    return steps


PHASES = {"prologue": [("T1", 0), ("QKV", 0), ("TK", 0), ("TQ", 0)], "first": batch_steps(False, True),
          "second": batch_steps(True, True), "loop": batch_steps(True, True), "last": batch_steps(True, False),
          "experts": expert_steps()}


def place_banks():
    places, at = {}, 0
    last = [None] * 5
    for phase, steps in PHASES.items():
        places[phase] = {}
        last = [(who, when - 1) for who, when in (x or (None, 0) for x in last)]
        for kind, n in steps:
            if kind == "Y":
                place = 3 + n // NT % 2
            elif kind in ("PV", "RL", "GT"):
                place = 3
            elif kind in ("TM", "TP", "PJ"):
                place = 4
            else:
                place, at = at, (at + 1) % 3
            places[phase][kind, n] = place, *last[place]
            last[place] = ((kind, n), 0)
    assert {u: p[0] for u, p in places["second"].items()} == {u: p[0] for u, p in places["loop"].items()}
    return places


PLACES = place_banks()


def attn_moe_kernel(nc, x, wq, wk, wv, wo, dirs, scale, wfc_s, bfc_s, wproj_s, bproj_s, wr, wfc, bfc,
                    wproj, bproj, out):
    with ExitStack() as ctx:
        def sb(name, shape, dt=F32):
            return ctx.enter_context(nc.sbuf_tensor(name, shape, dt))

        def sem(name):
            return ctx.enter_context(nc.semaphore(name))

        ident = sb("ident", [P, P])
        identb = sb("identb", [P, P], BF16)
        future = sb("future", [P, P], BF16)
        iota = sb("iota", [P, NE])
        wqkv = sb("wqkv", [P, 2 * H * QD + C])
        dirs_all = sb("dirs_all", [P, H * QD])
        scale_all = sb("scale_all", [P, 1])
        fold = sb("fold", [P, H * QD])
        dots = sb("dots", [P, H])
        wo_sb = sb("wo_sb", [P, C])
        wr_sb = sb("wr_sb", [P, NE])
        w1 = sb("w1", [P, NE + 1, HID])
        w1h = sb("w1h", [P, NE + 1, HID], F32R)
        w1l = sb("w1l", [P, NE + 1, HID], F32R)
        w2 = sb("w2", [P, NE + 1, NQ, C])
        b1rows = sb("b1rows", [(NE + 1) * NQ, P])
        b1 = sb("b1", [P, (NE + 1) * NQ])
        b2 = sb("b2", [NE + 1, C])
        xin = sb("xin", [P, NT, C])
        xres = sb("xres", [P, NT, C])
        stats = sb("stats", [P, NT, 6])
        meanvar = sb("meanvar", [P, NT, 2])
        rstd = sb("rstd", [P, NT])
        var_eps = sb("var_eps", [P, NT])
        half = sb("half", [P, NT])
        xn = sb("xn", [P, NT, C])
        xnT = sb("xnT", [P, T])
        parts = sb("parts", [P, NPART, 2, NT, H * QD], BF16)
        rest = sb("rest", [P, 2, NT, H * QD])
        qrows = sb("qrows", [P, NT, H, W], BF16)
        krows = sb("krows", [P, NT, H, W], BF16)
        kst = sb("kst", [P, G, T], BF16)
        qst = sb("qst", [P, G, T], BF16)
        qmst = sb("qmst", [P, 2, T], BF16)
        kpad = sb("kpad", [P, G, R, T], BF16)
        vext = sb("vext", [P, NT, H, W])
        negmax = sb("negmax", [P, G, NT, R])
        mrest = sb("mrest", [P, NT, R])
        probs = sb("probs", [P, 2, R, PW])
        vstage = sb("vstage", [P, NT, C])
        ot = sb("ot", [P, 2, T])
        rsum = sb("rsum", [P, NT, R])
        onorm = sb("onorm", [P, NT, C])
        onT = sb("onT", [P, T])
        x1 = sb("x1", [P, NT, C])
        x2n = sb("x2n", [P, NT, C])
        x2T = sb("x2T", [P, T])
        x2h = sb("x2h", [P, T], F32R)
        x2l = sb("x2l", [P, T], F32R)
        lneg = sb("lneg", [P, NT])
        lsh = sb("lsh", [P, NT, NE])
        pexp = sb("pexp", [P, NT, NE])
        psum_r = sb("psum_r", [P, NT])
        prcp = sb("prcp", [P, NT])
        pr = sb("pr", [P, NT, NE])
        top = sb("top", [P, NT, 8])
        topi = sb("topi", [P, NT, 8], U32)
        topf = sb("topf", [P, NT, 2])
        wsum = sb("wsum", [P, NT])
        wrcp = sb("wrcp", [P, NT])
        wtop = sb("wtop", [P, NT, 2])
        hot = sb("hot", [P, 2, NT, NE])
        gate = sb("gate", [P, NT, NE + 1])
        gateT = sb("gateT", [NE + 1, T])
        hidden = w1[:, 0:2 * NQ, :].rearrange("p (a q) t -> p a q t", a=2)
        acc = sb("acc", [P, NT, C])
        y = sb("y", [P, NT, C])

        banks = ctx.enter_context(nc.psum_tensor("banks", [P, 8, 512], F32))

        x_loaded, xres_loaded, proj_loaded, ffn_loaded = sem("x_loaded"), sem("xres_loaded"), sem("proj_loaded"), sem("ffn_loaded")
        kpad_loaded, out_stored = sem("kpad_loaded"), sem("out_stored")
        pool_made = sem("pool_made")
        consts_made = sem("consts_made")
        w1_split = sem("w1_split")
        proj_folded = sem("proj_folded")
        b1_turned, b1_ready = sem("b1_turned"), sem("b1_ready")
        var_ready, rstd_ready = sem("var_ready"), sem("rstd_ready")
        dve_step = sem("dve_step")
        ln1_done, xn_turned, xnT_ready = sem("ln1_done"), sem("xn_turned"), sem("xnT_ready")
        qkv_done, v_staged, v_ready, qkv_free, parts_ready = sem("qkv_done"), sem("v_staged"), sem("v_ready"), sem("qkv_free"), sem("parts_ready")
        k_spread, q_spread = sem("k_spread"), sem("q_spread")
        k_turned, q_turned, kst_ready, qst_ready = sem("k_turned"), sem("q_turned"), sem("kst_ready"), sem("qst_ready")
        m_scores, m_taken, m_parts = sem("m_scores"), sem("m_taken"), sem("m_parts")
        qm_turned, qmst_ready = sem("qm_turned"), sem("qmst_ready")
        scores_ready, exp_done, masked = sem("scores_ready"), sem("exp_done"), sem("masked")
        pv_done, ot_ready, ot_turned, onorm_ready = sem("pv_done"), sem("ot_ready"), sem("ot_turned"), sem("onorm_ready")
        on_turned, onT_ready, proj_done, x1_ready = sem("on_turned"), sem("onT_ready"), sem("proj_done"), sem("x1_ready")
        ln2_done, x2_turned, x2T_ready, x2_split = sem("ln2_done"), sem("x2_turned"), sem("x2T_ready"), sem("x2_split")
        logits_done, logits_taken, pexp_ready = sem("logits_done"), sem("logits_taken"), sem("pexp_ready")
        gates_ready, gate_turned, gateT_ready = sem("gates_ready"), sem("gate_turned"), sem("gateT_ready")
        h_ready, gelu_done, y_done, y_taken, out_ready = sem("h_ready"), sem("gelu_done"), sem("y_done"), sem("y_taken"), sem("out_ready")

        PROJ_LOADS, FFN_LOADS = 6, 8

        def ring(slot):
            return banks[:, 2 * slot:2 * slot + 2, :]

        def flat(slot):
            return ring(slot).rearrange("p a c -> p (a c)")

        def unit_view(slot, tiles):
            if tiles >= 3:
                return ring(slot)[:, :, 0:P * tiles]
            if tiles == 2:
                return flat(slot).rearrange("p (n w) -> p n w", w=2 * P)
            return banks[:, 2 * slot, :].rearrange("p (n w) -> p n w", w=P)

        def opens_bank(tiles, n):
            return tiles >= 3 or (tiles == 2 and n % 2 == 0) or n == 0

        def six(cols=512):
            return banks[:, 6, 0:cols]

        def seven(cols=512):
            return banks[:, 7, 0:cols]

        def y_bank(e):
            return banks[:, 6 + e % 2, :].rearrange("p (i c) -> p i c", i=NT)

        def wait_earlier(eng, semaphore, value):
            if not isinstance(value, int) or value > 0:
                eng.wait_ge(semaphore, value)

        def wait_apart(eng, semaphore, value):
            eng.wait_ge(consts_made, 1)
            eng.wait_ge(semaphore, value)

        def batch_loop(eng, body):
            body(0, "first", False, True)
            body(1, "second", True, True)
            with eng.Fori(2, B - 1) as b:
                body(b, "loop", True, True)
            body(B - 1, "last", True, False)

        block = ctx.enter_context(nc.Block())

        @block.sync
        def _(sp):
            xv = x.rearrange("b (i p) c -> p (b i) c", p=P)
            ov = out.rearrange("b (i p) c -> p (b i) c", p=P)
            sp.dma_start(xin[:], xv[:, 0:NT, :]).then_inc(x_loaded, 16)
            sp.dma_start(wqkv[:, 0:48], wq).then_inc(proj_loaded, 16)
            sp.dma_start(wqkv[:, 48:96], wk).then_inc(proj_loaded, 16)
            sp.dma_start(wqkv[:, 96:224], wv).then_inc(proj_loaded, 16)
            sp.dma_start(dirs_all[:], dirs.rearrange("(o h) d -> o (h d)", o=1).partition_broadcast(P)).then_inc(proj_loaded, 16)
            sp.dma_start(scale_all[:], scale.rearrange("(o h) -> o h", o=1).partition_broadcast(P)).then_inc(proj_loaded, 16)
            sp.dma_start(wo_sb[:], wo).then_inc(proj_loaded, 16)
            sp.dma_start(w1[:, 0:NE, :], wfc.rearrange("e c h -> c e h")).then_inc(ffn_loaded, 16)
            sp.dma_start(w1[:, NE, :], wfc_s).then_inc(ffn_loaded, 16)
            sp.dma_start(w2[:, 0:NE].rearrange("p e q n -> p (e q) n"), wproj.rearrange("e (q p) n -> p (e q) n", p=P)).then_inc(ffn_loaded, 16)
            sp.dma_start(w2[:, NE], wproj_s.rearrange("(q p) n -> p q n", p=P)).then_inc(ffn_loaded, 16)
            sp.dma_start(b1rows[0:NE * NQ, :], bfc.rearrange("e (q p) -> (e q) p", p=P)).then_inc(ffn_loaded, 16)
            sp.dma_start(b1rows[NE * NQ:(NE + 1) * NQ, :], bfc_s.rearrange("(q p) -> q p", p=P)).then_inc(ffn_loaded, 16)
            sp.dma_start(b2[0:NE, :], bproj).then_inc(ffn_loaded, 16)
            sp.dma_start(b2[NE:NE + 1, :], bproj_s.rearrange("(o n) -> o n", o=1)).then_inc(ffn_loaded, 16)
            sp.dma_start(wr_sb[:], wr).then_inc(ffn_loaded, 16)

            def spread_k(bb):
                wait_apart(sp, kst_ready, bb + 1)
                for r in range(R):
                    sp.dma_start(kpad[W * r:W * r + W, :, r, :], kst[W * r:W * r + W, :, :]).then_inc(kpad_loaded, 16)

            def store(f):
                sp.dma_start(ov[:, bass.ds(f * NT, NT), :], y[:]).then_inc(out_stored, 16)

            def body(b, phase, experts, prepare):
                if prepare:
                    wait_apart(sp, ln1_done, b + 1)
                    sp.dma_start(xin[:], xv[:, bass.ds(b * NT + NT, NT), :]).then_inc(x_loaded, 16)
                if experts:
                    wait_apart(sp, x1_ready, b)
                sp.dma_start(xres[:], xv[:, bass.ds(b * NT, NT), :]).then_inc(xres_loaded, 16)
                if prepare:
                    spread_k(b + 1)
                if experts:
                    wait_apart(sp, out_ready, b)
                    store(b - 1)

            sp.wait_ge(consts_made, 1)
            spread_k(0)
            batch_loop(sp, body)
            sp.wait_ge(out_ready, B)
            store(B - 1)
            sp.wait_ge(out_stored, 16 * B)

        @block.gpsimd
        def _(pool):
            made = 0
            unit_seen = pool.alloc_register("unit_seen")
            batch_seen = pool.alloc_register("batch_seen")
            group_seen = pool.alloc_register("group_seen")
            batch_next = pool.alloc_register("batch_next")
            for counter in (unit_seen, batch_seen, group_seen):
                pool.reg_mov(counter, 0)
            pool.reg_mov(batch_next, 1)

            def link(ins):
                nonlocal made
                made += 1
                ins.then_inc(pool_made, 1)
                pool.wait_ge(pool_made, made)

            def root(nth):
                pool.wait_ge(var_ready, nth)
                pool.tensor_tensor(rstd[:], var_eps[:], half[:], ALU.pow).then_inc(rstd_ready, 1)

            pool.memset(ident[:], 0.0)
            pool.memset(identb[:], 0.0)
            pool.memset(future[:], 0.0)
            pool.memset(qrows[:], 0.0)
            pool.memset(krows[:], 0.0)
            link(pool.memset(vext[:], 0.0))
            for m in (ident, identb):
                pool.affine_select(out=m[:], in_=m[:], compare_op=ALU.not_equal, fill=1.0, base=0,
                                   pattern=[[-1, P]], channel_multiplier=1)
            pool.affine_select(out=future[:], in_=future[:], compare_op=ALU.is_ge, fill=NEG, base=0,
                               pattern=[[-1, P]], channel_multiplier=1)
            pool.memset(vext[:, :, :, HD:HD + 1], 1.0)
            pool.memset(gate[:], 1.0)
            link(pool.memset(half[:], -0.5))
            root(1)
            pool.memset(krows[:, :, :, 0:NPART], 1.0)
            pool.memset(kpad[:].rearrange("p g r t -> p (g r t)").bitcast(F32), 0.0).then_inc(consts_made, 1)

            def spread_parts(first=False):
                if first:
                    pool.wait_ge(parts_ready, 1)
                else:
                    pool.reg_add(batch_seen, batch_seen, 1)
                    pool.reg_add(batch_next, batch_next, 1)
                    pool.reg_add(group_seen, group_seen, G)
                    pool.wait_ge(consts_made, 1)
                    pool.wait_ge(parts_ready, batch_next)
                    pool.wait_ge(k_turned, batch_seen)
                qv = qrows[:].rearrange("p i h s -> p (i h) s")
                kv = krows[:].rearrange("p i h s -> p (i h) s")

                def part(n, which):
                    v = parts[:, n, which].rearrange("p i (h d) -> p (i h) d", d=QD)
                    return v.unsqueeze(2).to_broadcast([P, NT * H, NPART, QD])

                for c in range(NPART):
                    dst = kv[:, :, SLOT0:SLOT0 + 27].rearrange("p h (a c d) -> p h a c d", a=NPART, c=NPART)[:, :, :, c, :]
                    last = pool.tensor_copy(dst, part(c, 1))
                last.then_inc(k_spread, 1)
                if not first:
                    pool.wait_ge(consts_made, 1)
                    pool.wait_ge(qm_turned, group_seen)
                pool.memset(qv[:, :, 0:NPART], 0.0)
                for a in range(NPART):
                    dst = qv[:, :, SLOT0 + 9 * a:SLOT0 + 9 * a + 9].rearrange("p h (c d) -> p h c d", c=NPART)
                    last = pool.tensor_copy(dst, part(a, 0))
                last.then_inc(q_spread, 1)

            def place_values():
                pool.wait_ge(consts_made, 1)
                pool.wait_ge(v_staged, batch_next)
                pool.wait_ge(pv_done, group_seen)
                pool.tensor_copy(vext[:, :, :, 0:HD], vstage[:].rearrange("p i (h d) -> p i h d", d=HD)).then_inc(v_ready, 1)

            def mask_probs(b, g):
                for k, (tiles, heads) in enumerate(UNITS):
                    pool.reg_add(unit_seen, unit_seen, 1)
                    pool.wait_ge(consts_made, 1)
                    pool.wait_ge(exp_done, unit_seen)
                    v = probs[:, g % 2, heads[0]:heads[-1] + 1, PCOL[tiles]:PCOL[tiles] + P]
                    pool.affine_select(out=v, in_=v, compare_op=ALU.is_ge, fill=0.0, base=0,
                                       pattern=[[0, len(heads)], [1, P]], channel_multiplier=-1).then_inc(masked, 1)

            def body(b, phase, experts, prepare):
                mask_probs(b, 0)
                if prepare:
                    root(2 * b + 2)
                mask_probs(b, 1)
                mask_probs(b, 2)
                if prepare:
                    spread_parts()
                mask_probs(b, 3)
                if prepare:
                    place_values()
                root(2 * b + (3 if prepare else 2))

            spread_parts(first=True)
            pool.wait_ge(v_staged, 1)
            pool.tensor_copy(vext[:, :, :, 0:HD], vstage[:].rearrange("p i (h d) -> p i h d", d=HD)).then_inc(v_ready, 1)
            pool.wait_ge(ffn_loaded, 16 * 9)
            for e in range(NE + 1):
                pool.tensor_copy(w1h[:, e, :], w1[:, e, :]).then_inc(pool_made, 1)
                made += 1
            for e in range(NE + 1):
                pool.wait_ge(pool_made, made - NE + e)
                pool.tensor_tensor(w1l[:, e, :], w1[:, e, :], w1h[:, e, :].bitcast(F32), ALU.subtract).then_inc(w1_split, 1)
            batch_loop(pool, body)

        @block.scalar
        def _(act):
            def copy(dst, src):
                return nc.scalar.activation(dst, src, ACT.Copy)

            def evacuate_xn(bb, place):
                act.wait_ge(xn_turned, bb + 1)
                wait_earlier(act, qkv_done, bb)
                copy(xnT[:], flat(place)[:, 0:T]).then_inc(xnT_ready, 1)

            def stage_v(bb, place):
                act.wait_ge(qkv_done, bb + 1)
                wait_earlier(act, v_ready, bb)
                src = flat(place).rearrange("p (i c) -> p i c", i=NT)[:, :, 96:224]
                copy(vstage[:], src).then_inc(v_staged, 1)

            def evacuate_k(bb, place):
                act.wait_ge(k_turned, bb + 1)
                wait_earlier(act, kpad_loaded, bb * 16 * R)
                copy(kst[:].rearrange("p g t -> p (g t)"), flat(place).bitcast(BF16)).then_inc(kst_ready, 1)

            def evacuate_q(bb, place):
                act.wait_ge(q_turned, bb + 1)
                wait_earlier(act, m_scores, bb * M_PER)
                copy(qst[:].rearrange("p g t -> p (g t)"), flat(place).bitcast(BF16)).then_inc(qst_ready, 1)

            def exps(b, g, at):
                for k, (tiles, heads) in enumerate(UNITS):
                    act.wait_ge(scores_ready, b * E_PER + g * NU + k + 1)
                    wait_earlier(act, pv_done, b * G + max(0, g - 1))
                    nc.scalar.activation(probs[:, g % 2, heads[0]:heads[-1] + 1, PCOL[tiles]:PCOL[tiles] + P * tiles],
                                         unit_view(at["E", g * NU + k][0], tiles), ACT.Exp).then_inc(exp_done, 1)

            def evacuate_o(b, g):
                act.wait_ge(pv_done, b * G + g + 1)
                wait_earlier(act, ot_turned, b * G + max(0, g - 1))
                copy(ot[:, g % 2, :], six()).then_inc(ot_ready, 1)

            def gelus(f, e, at):
                for q in range(NQ):
                    if q % 2 == 0:
                        act.wait_ge(h_ready, f * 2 * (NE + 1) + 2 * e + q // 2 + 1)
                    if q == 0:
                        wait_earlier(act, y_done, f * Y_PER + max(0, e - 1))
                    nc.scalar.activation(hidden[:, e % 2, q, :], ring(at["H", 2 * e + q // 2][0])[:, q % 2, :],
                                         ACT.Gelu_apprx_tanh, bias=b1[:, e * NQ + q:e * NQ + q + 1]).then_inc(gelu_done, 1)

            def evacuate_gates(f):
                act.wait_ge(gate_turned, f + 1)
                copy(gateT[:], six()[0:NE + 1, :]).then_inc(gateT_ready, 1)

            def body(b, phase, experts, prepare):
                at = PLACES[phase]
                for g in range(G):
                    if experts:
                        gelus(b - 1, 2 * g, at)
                    if g >= 2:
                        evacuate_o(b, g - 2)
                    if experts:
                        if g == 1:
                            evacuate_gates(b - 1)
                        gelus(b - 1, 2 * g + 1, at)
                    if prepare and g == 1:
                        evacuate_xn(b + 1, at["T1", 0][0])
                    if prepare and g == 2:
                        stage_v(b + 1, at["QKV", 0][0])
                    exps(b, g, at)
                evacuate_o(b, G - 2)
                evacuate_o(b, G - 1)
                if experts:
                    gelus(b - 1, NE, at)
                act.wait_ge(on_turned, b + 1)
                copy(onT[:], flat(at["TO", 0][0])[:, 0:T]).then_inc(onT_ready, 1)
                if prepare:
                    evacuate_k(b + 1, at["TK", 0][0])
                    evacuate_q(b + 1, at["TQ", 0][0])
                act.wait_ge(x2_turned, b + 1)
                copy(x2T[:], flat(at["T2", 0][0])[:, 0:T]).then_inc(x2T_ready, 1)
                act.wait_ge(logits_taken, b + 1)
                nc.scalar.activation(pexp[:], lsh[:], ACT.Exp).then_inc(pexp_ready, 1)

            at = PLACES["prologue"]
            evacuate_xn(0, at["T1", 0][0])
            stage_v(0, at["QKV", 0][0])
            evacuate_k(0, at["TK", 0][0])
            evacuate_q(0, at["TQ", 0][0])
            act.wait_ge(b1_ready, 1)
            batch_loop(act, body)
            for e in range(NE + 1):
                gelus(B - 1, e, PLACES["experts"])
                if e == 3:
                    evacuate_gates(B - 1)

        @block.vector
        def _(dve):
            class Chain:

                def __init__(self):
                    dve.sem_clear(dve_step)
                    self.n = 0

                def __call__(self, ins):
                    self.n += 1
                    ins.then_inc(dve_step, 1)
                    dve.wait_ge(dve_step, self.n)

            def bc(ap, n):
                shape = list(ap.shape) + [n]
                return ap.unsqueeze(len(ap.shape)).to_broadcast(shape)

            def layernorm(link, dst, src, nth):
                for i in range(NT):
                    last = dve.bn_stats(stats[:, i, :], src[:, i, :])
                link(last)
                for i in range(NT):
                    last = dve.bn_aggr(meanvar[:, i, :], stats[:, i, :])
                link(last)
                dve.tensor_scalar(var_eps[:], meanvar[:, :, 1], EPS, None, ALU.add).then_inc(var_ready, 1)
                dve.wait_ge(rstd_ready, nth)
                for i in range(NT):
                    last = dve.tensor_scalar(dst[:, i, :], src[:, i, :], meanvar[:, i, 0:1], rstd[:, i:i + 1],
                                             ALU.subtract, ALU.mult)
                return last

            def first_norm(bb, link, nth):
                dve.wait_ge(x_loaded, bb * 16 + 16)
                wait_earlier(dve, xn_turned, bb)
                layernorm(link, xn, xin, nth).then_inc(ln1_done, 1)

            def split_qk(bb, link, place):
                dve.wait_ge(v_staged, bb + 1)
                wait_earlier(dve, q_spread, bb)
                qk = flat(place).rearrange("p (i c) -> p i c", i=NT)[:, :, 0:96].rearrange("p i (w c) -> p w i c", w=2)
                link(dve.tensor_copy(parts[:, 0], qk))
                dve.tensor_tensor(rest[:], qk, parts[:, 0], ALU.subtract).then_inc(qkv_free, 1)
                dve.wait_ge(qkv_free, bb + 1)
                link(dve.tensor_copy(parts[:, 1], rest[:]))
                dve.tensor_tensor(parts[:, 2], rest[:], parts[:, 1], ALU.subtract).then_inc(parts_ready, 1)

            def take_maxima(b, g, at):
                for k, (tiles, heads) in enumerate(UNITS):
                    dve.wait_ge(m_scores, b * M_PER + g * NU + k + 1)
                    dve.tensor_reduce(negmax[:, g, tiles - 1, heads[0]:heads[-1] + 1], unit_view(at["M", g * NU + k][0], tiles),
                                      AX.X, ALU.max, negate=True).then_inc(m_taken, 1)

            def split_maxima(b, g, link):
                dve.wait_ge(m_taken, b * M_PER + g * NU + NU)
                dst = qrows[:, :, R * g:R * g + R, :]
                link(dve.tensor_copy(dst[:, :, :, 0], negmax[:, g]))
                link(dve.tensor_tensor(mrest[:], negmax[:, g], dst[:, :, :, 0], ALU.subtract))
                link(dve.tensor_copy(dst[:, :, :, 1], mrest[:]))
                dve.tensor_tensor(dst[:, :, :, 2], mrest[:], dst[:, :, :, 1], ALU.subtract).then_inc(m_parts, 1)

            def evacuate_qm(b, g):
                dve.wait_ge(qm_turned, b * G + g + 1)
                wait_earlier(dve, scores_ready, b * E_PER + NU * max(0, g - 1))
                dve.tensor_copy(qmst[:, g % 2, :], seven(256).bitcast(BF16)).then_inc(qmst_ready, 1)

            def normalize(b, g, link):
                dve.wait_ge(ot_turned, b * G + g + 1)
                src = seven().rearrange("p (i r w) -> p i r w", i=NT, r=R)
                link(dve.reciprocal(rsum[:], src[:, :, :, HD]))
                dst = onorm[:].rearrange("p i (g r d) -> p i g r d", g=G, r=R)[:, :, g]
                dve.tensor_tensor(dst, src[:, :, :, 0:HD], bc(rsum[:], HD), ALU.mult).then_inc(onorm_ready, 1)

            def route(b, link):
                dve.wait_ge(logits_done, b + 1)
                logits = six(NT * NE).rearrange("p (i e) -> p i e", i=NT)
                link(dve.tensor_reduce(lneg[:], logits, AX.X, ALU.max, negate=True))
                dve.tensor_tensor(lsh[:], logits, bc(lneg[:], NE), ALU.add).then_inc(logits_taken, 1)
                dve.wait_ge(pexp_ready, b + 1)
                link(dve.tensor_reduce(psum_r[:], pexp[:], AX.X, ALU.add))
                link(dve.reciprocal(prcp[:], psum_r[:]))
                link(dve.tensor_tensor(pr[:], pexp[:], bc(prcp[:], NE), ALU.mult))
                for i in range(NT):
                    last = dve.max(top[:, i, :], pr[:, i, :])
                link(last)
                for i in range(NT):
                    last = dve.max_index(topi[:, i, :], top[:, i, :], pr[:, i, :])
                dve.tensor_tensor(wsum[:], top[:, :, 0], top[:, :, 1], ALU.add)
                link(last)
                link(dve.tensor_copy(topf[:], topi[:, :, 0:2]))
                link(dve.reciprocal(wrcp[:], wsum[:]))
                link(dve.tensor_tensor(wtop[:], top[:, :, 0:2], bc(wrcp[:], 2), ALU.mult))
                every = iota[:].unsqueeze(1).to_broadcast([P, NT, NE])
                for n in range(2):
                    last = dve.tensor_tensor(hot[:, n], every, bc(topf[:, :, n], NE), ALU.is_equal)
                link(last)
                for n in range(2):
                    last = dve.tensor_tensor(hot[:, n], hot[:, n], bc(wtop[:, :, n], NE), ALU.mult)
                link(last)
                dve.tensor_tensor(gate[:, :, 0:NE], hot[:, 0], hot[:, 1], ALU.add).then_inc(gates_ready, 1)

            def add_expert(f, e):
                dve.wait_ge(y_done, f * Y_PER + e + 1)
                src = y_bank(e)
                if e == NE:
                    dve.wait_ge(y_taken, f * NE + e)
                    wait_earlier(dve, out_stored, f * 16)
                    dve.tensor_tensor(y[:], src, acc[:], ALU.add).then_inc(out_ready, 1)
                    return
                dve.wait_ge(gates_ready, f + 1)
                if e > 0:
                    dve.wait_ge(y_taken, f * NE + e)
                for i in range(NT):
                    last = dve.scalar_tensor_tensor(acc[:, i, :], src[:, i, :], gate[:, i, e:e + 1],
                                                    (acc if e else x1)[:, i, :], ALU.mult, ALU.add)
                last.then_inc(y_taken, 1)

            def residual(b):
                dve.wait_ge(proj_done, b + 1)
                dve.wait_ge(xres_loaded, b * 16 + 16)
                dve.tensor_tensor(x1[:], banks[:, 7, :].rearrange("p (i c) -> p i c", i=NT), xres[:], ALU.add).then_inc(x1_ready, 1)

            def body(b, phase, experts, prepare):
                at = PLACES[phase]
                link = Chain()
                take_maxima(b, 0, at)
                split_maxima(b, 0, link)
                evacuate_qm(b, 0)
                for g in range(G - 1):
                    take_maxima(b, g + 1, at)
                    split_maxima(b, g + 1, link)
                    if experts:
                        add_expert(b - 1, 2 * g)
                        add_expert(b - 1, 2 * g + 1)
                    evacuate_qm(b, g + 1)
                    if g >= 1:
                        normalize(b, g - 1, link)
                    if prepare and g == 0:
                        first_norm(b + 1, link, 2 * b + 2)
                    if prepare and g == 1:
                        split_qk(b + 1, link, at["QKV", 0][0])
                if experts:
                    add_expert(b - 1, 2 * G - 2)
                    add_expert(b - 1, 2 * G - 1)
                normalize(b, G - 2, link)
                normalize(b, G - 1, link)
                residual(b)
                dve.wait_ge(x1_ready, b + 1)
                layernorm(link, x2n, x1, 2 * b + (3 if prepare else 2)).then_inc(ln2_done, 1)
                if experts:
                    add_expert(b - 1, NE)
                dve.wait_ge(x2T_ready, b + 1)
                link(dve.tensor_copy(x2h[:], x2T[:]))
                dve.tensor_tensor(x2l[:], x2T[:], x2h[:].bitcast(F32), ALU.subtract).then_inc(x2_split, 1)
                route(b, link)

            link = Chain()
            first_norm(0, link, 1)
            dve.wait_ge(proj_loaded, 16 * PROJ_LOADS)
            wk3 = wqkv[:, 48:96]
            link(dve.tensor_tensor(fold[:], wk3, dirs_all[:], ALU.mult))
            link(dve.tensor_reduce(dots[:], fold[:].rearrange("p (h d) -> p h d", d=QD), AX.X, ALU.add))
            link(dve.tensor_tensor(fold[:].rearrange("p (h d) -> p h d", d=QD), dirs_all[:].rearrange("p (h d) -> p h d", d=QD),
                                   bc(dots[:], QD), ALU.mult))
            dve.scalar_tensor_tensor(wk3, wk3, scale_all[:, 0:1], fold[:], ALU.mult, ALU.add).then_inc(proj_folded, 1)
            for e in range(NE):
                dve.memset(iota[:, e:e + 1], float(e))
            split_qk(0, link, PLACES["prologue"]["QKV", 0][0])
            dve.wait_ge(b1_turned, 1)
            dve.tensor_copy(b1[:], banks[:, 6, 0:(NE + 1) * NQ]).then_inc(b1_ready, 1)
            dve.wait_ge(b1_ready, 1)
            batch_loop(dve, body)
            for e in range(NE + 1):
                add_expert(B - 1, e)

        @block.tensor
        def _(pe):
            mm = nc.tensor.matmul

            def turn(dst, src, eye):
                return nc.tensor.transpose(dst, src, eye)

            def turn_xn(bb, place):
                pe.wait_ge(ln1_done, bb + 1)
                for i in range(NT):
                    last = turn(flat(place)[:, P * i:P * i + P], xn[:, i, :], ident[:])
                last.then_inc(xn_turned, 1)

            def project(bb, place):
                pe.wait_ge(xnT_ready, bb + 1)
                for i in range(NT):
                    last = mm(flat(place)[:, 2 * P * i:2 * P * i + 224], xnT[:, P * i:P * i + P], wqkv[:], start=True, stop=True)
                last.then_inc(qkv_done, 1)

            def turn_stacks(bb, place, rows, spread, turned):
                pe.wait_ge(spread, bb + 1)
                dst = flat(place).bitcast(BF16)
                for g in range(G):
                    for i in range(NT):
                        last = turn(dst[:, T * g + P * i:T * g + P * i + P],
                                    rows[:, i, R * g:R * g + R, :].rearrange("p h s -> p (h s)"), identb[:])
                last.then_inc(turned, 1)

            def max_scores(b, n, place):
                g, (tiles, heads) = n // NU, UNITS[n % NU]
                if n == 0:
                    pe.wait_ge(kpad_loaded, b * 16 * R + 16 * R)
                    pe.wait_ge(qst_ready, b + 1)
                dst, i = unit_view(place, tiles), tiles - 1
                for m, r in enumerate(heads):
                    mm(dst[:, m, :], qst[:, g, P * i:P * i + P], kpad[:, g, r, 0:P * tiles],
                       start=opens_bank(tiles, m), stop=False, skip_group_check=True)
                    last = mm(dst[:, m, P * i:P * i + P], identb[:], future[:], start=False, stop=True,
                              skip_group_check=True)
                last.then_inc(m_scores, 1)

            def scores(b, n, place):
                g, (tiles, heads) = n // NU, UNITS[n % NU]
                if n % NU == 0:
                    pe.wait_ge(qmst_ready, b * G + g + 1)
                dst, j = unit_view(place, tiles), NT - tiles
                for m, r in enumerate(heads):
                    last = mm(dst[:, m, :], kpad[:, g, r, P * j:P * j + P], qmst[:, g % 2, P * j:T],
                              start=opens_bank(tiles, m), stop=True, skip_group_check=True)
                last.then_inc(scores_ready, 1)

            def turn_maxima(b, g):
                pe.wait_ge(m_parts, b * G + g + 1)
                dst = seven(256).bitcast(BF16)
                for i in range(NT):
                    last = turn(dst[:, P * i:P * i + P], qrows[:, i, R * g:R * g + R, :].rearrange("p h s -> p (h s)"),
                                identb[:])
                last.then_inc(qm_turned, 1)

            def values(b, g):
                pe.wait_ge(masked, b * E_PER + g * NU + NU)
                if g == 0:
                    pe.wait_ge(v_ready, b + 1)
                for j in range(NT):
                    tiles = NT - j
                    for r in range(R):
                        last = mm(banks[W * r:W * r + W, 6, P * j:T], vext[:, j, R * g + r, :],
                                  probs[:, g % 2, r, PCOL[tiles]:PCOL[tiles] + P * tiles], start=(j == 0), stop=(j == NT - 1))
                last.then_inc(pv_done, 1)

            def turn_values(b, g):
                pe.wait_ge(ot_ready, b * G + g + 1)
                for i in range(NT):
                    last = turn(seven()[:, P * i:P * i + P], ot[:, g % 2, P * i:P * i + P], ident[:])
                last.then_inc(ot_turned, 1)

            def turn_heads(b, place):
                pe.wait_ge(onorm_ready, b * G + G)
                for i in range(NT):
                    last = turn(flat(place)[:, P * i:P * i + P], onorm[:, i, :], ident[:])
                last.then_inc(on_turned, 1)

            def project_out(b):
                pe.wait_ge(onT_ready, b + 1)
                for i in range(NT):
                    last = mm(seven()[:, P * i:P * i + P], onT[:, P * i:P * i + P], wo_sb[:], start=True, stop=True)
                last.then_inc(proj_done, 1)

            def turn_x2(b, place):
                pe.wait_ge(ln2_done, b + 1)
                for i in range(NT):
                    last = turn(flat(place)[:, P * i:P * i + P], x2n[:, i, :], ident[:])
                last.then_inc(x2_turned, 1)

            def logits(b):
                pe.wait_ge(x2T_ready, b + 1)
                for i in range(NT):
                    last = mm(six()[:, NE * i:NE * i + NE], x2T[:, P * i:P * i + P], wr_sb[:], start=True, stop=True)
                last.then_inc(logits_done, 1)

            def first_layer(f, n, place):
                e, u = n // 2, n % 2
                if n == 0:
                    pe.wait_ge(x2_split, f + 1)
                for q in (2 * u, 2 * u + 1):
                    dst = ring(place)[:, q % 2, :]
                    wh, wl = w1h[:, e, P * q:P * q + P], w1l[:, e, P * q:P * q + P]
                    mm(dst, wh, x2h[:], start=True, stop=False)
                    mm(dst, wh, x2l[:], start=False, stop=False)
                    last = mm(dst, wl, x2h[:], start=False, stop=True)
                last.then_inc(h_ready, 1)

            def second_layer(f, n):
                e, i = n // NT, n % NT
                if i == 0:
                    pe.wait_ge(gelu_done, f * GELU_PER + NQ * e + NQ)
                for q in range(NQ):
                    last = mm(y_bank(e)[:, i, :], hidden[:, e % 2, q, P * i:P * i + P], w2[:, e, q, :],
                              start=(q == 0), stop=(q == NQ - 1 and e < NE))
                if e == NE:
                    if i == 0:
                        pe.wait_ge(gateT_ready, f + 1)
                    last = mm(y_bank(e)[:, i, :], gateT[:, P * i:P * i + P], b2[:], start=False, stop=True)
                if i == NT - 1:
                    last.then_inc(y_done, 1)

            def turn_gates(f):
                pe.wait_ge(gates_ready, f + 1)
                for i in range(NT):
                    last = turn(six()[0:NE + 1, P * i:P * i + P], gate[:, i, :], ident[:])
                last.then_inc(gate_turned, 1)

            def wait_read(b, unit, when):
                if unit is None:
                    return
                kind, n = unit
                a, f, bb = b + when, b - 1 + when, b + 1 + when
                if kind == "M":
                    pe.wait_ge(m_taken, a * M_PER + n + 1)
                elif kind == "E":
                    pe.wait_ge(exp_done, a * E_PER + n + 1)
                elif kind == "TO":
                    pe.wait_ge(onT_ready, a + 1)
                elif kind == "T2":
                    pe.wait_ge(x2T_ready, a + 1)
                elif kind == "TM":
                    pe.wait_ge(qmst_ready, a * G + n + 1)
                elif kind == "PV":
                    pe.wait_ge(ot_ready, a * G + n + 1)
                elif kind == "TP":
                    pe.wait_ge(onorm_ready, a * G + n + 1)
                elif kind == "PJ":
                    pe.wait_ge(x1_ready, a + 1)
                elif kind == "RL":
                    pe.wait_ge(logits_taken, a + 1)
                elif kind == "H":
                    pe.wait_ge(gelu_done, f * GELU_PER + 2 * (n + 1))
                elif kind == "GT":
                    pe.wait_ge(gateT_ready, f + 1)
                elif kind == "Y" and n // NT < NE:
                    pe.wait_ge(y_taken, f * NE + n // NT + 1)
                elif kind == "Y":
                    pe.wait_ge(out_ready, f + 1)
                elif kind == "T1":
                    pe.wait_ge(xnT_ready, bb + 1)
                elif kind == "QKV":
                    pe.wait_ge(qkv_free, bb + 1)
                elif kind == "TK":
                    pe.wait_ge(kst_ready, bb + 1)
                elif kind == "TQ":
                    pe.wait_ge(qst_ready, bb + 1)

            def run(b, phase):
                for (kind, n) in PHASES[phase]:
                    place, unit, when = PLACES[phase][kind, n]
                    if not (kind == "Y" and n % NT):
                        wait_read(b, unit, when)
                    if kind == "M":
                        max_scores(b, n, place)
                    elif kind == "E":
                        scores(b, n, place)
                    elif kind == "TM":
                        turn_maxima(b, n)
                    elif kind == "PV":
                        values(b, n)
                    elif kind == "TP":
                        turn_values(b, n)
                    elif kind == "TO":
                        turn_heads(b, place)
                    elif kind == "PJ":
                        project_out(b)
                    elif kind == "T2":
                        turn_x2(b, place)
                    elif kind == "RL":
                        logits(b)
                    elif kind == "H":
                        first_layer(b - 1, n, place)
                    elif kind == "Y":
                        second_layer(b - 1, n)
                    elif kind == "GT":
                        turn_gates(b - 1)
                    elif kind == "T1":
                        turn_xn(b + 1, place)
                    elif kind == "QKV":
                        project(b + 1, place)
                    elif kind == "TK":
                        turn_stacks(b + 1, place, krows, k_spread, k_turned)
                    elif kind == "TQ":
                        turn_stacks(b + 1, place, qrows, q_spread, q_turned)

            pe.wait_ge(consts_made, 1)
            pe.wait_ge(ffn_loaded, 16 * 9)
            turn(banks[:, 6, 0:(NE + 1) * NQ], b1rows[:], ident[0:(NE + 1) * NQ, 0:(NE + 1) * NQ]).then_inc(b1_turned, 1)
            pe.wait_ge(proj_folded, 1)
            run(-1, "prologue")
            pe.wait_ge(b1_ready, 1)
            run(0, "first")
            pe.wait_ge(w1_split, NE + 1)
            run(1, "second")
            with pe.Fori(2, B - 1) as b:
                run(b, "loop")
            run(B - 1, "last")
            run(B, "experts")


_INS = ["L0_attn_x", "L0_attn_wq", "L0_attn_wk", "L0_attn_wv", "L0_attn_wo", "L0_attn_head_dirs", "L0_attn_scale",
        "L0_ffn_Wfc_s", "L0_ffn_bfc_s", "L0_ffn_Wproj_s", "L0_ffn_bproj_s", "L0_ffn_Wr", "L0_ffn_Wfc", "L0_ffn_bfc",
        "L0_ffn_Wproj", "L0_ffn_bproj"]


def kernel(**inputs):
    import numpy as _np
    import concourse.bacc as _bacc
    from concourse import mybir as _mybir
    from concourse.bass_utils import run_bass_kernel_spmd as _run

    nc = _bacc.Bacc("TRN2", target_bir_lowering=False, num_devices=1)
    arrays, args = {}, []
    for name in _INS:
        a = _np.ascontiguousarray(inputs[name])
        arrays[f"in_{name}"] = a
        args.append(nc.dram_tensor(f"in_{name}", a.shape, _mybir.dt.from_np(a.dtype), kind="ExternalInput").ap())
    args.append(nc.dram_tensor("out_0", (B, T, C), _mybir.dt.float32, kind="ExternalOutput").ap())
    attn_moe_kernel(nc, *args)
    r = _run(nc, [arrays], core_ids=[0])
    return r.results[0]["out_0"]
```

```python
from contextlib import ExitStack

import concourse.bass as bass
from concourse import mybir

F32 = mybir.dt.float32
F32R = mybir.dt.float32r
BF16 = mybir.dt.bfloat16
U32 = mybir.dt.uint32
ALU = mybir.AluOpType
ACT = mybir.ActivationFunctionType
AX = mybir.AxisListType

P = 128
B, T, C = 8, 512, 128
H, HD, QD = 16, 8, 3
NT = T // P
R = 4
G = H // R
W = P // R
NE = 8
HID = 512
NQ = HID // P
EPS = 1e-5
NEG = -1e30

NPART = 3
SLOT0 = NPART

UNITS = [(4, (0, 1)), (4, (2, 3)), (3, (0, 1)), (3, (2, 3)), (2, (0, 1, 2, 3)), (1, (0, 1, 2, 3))]
NU = len(UNITS)
PCOL = {4: 0, 3: 512, 2: 896, 1: 1152}
PW = 1280

M_PER, E_PER, Y_PER, GELU_PER = G * NU, G * NU, NE + 1, (NE + 1) * NQ

TENSOR_ORDER = """
    M.0 M.1 H.0 H.1 H.2 M.2 M.3 Y.0 M.4 Y.1 M.5 H.3 Y.2 TM.0 M.6 M.7 M.8 Y.3 E.0 Y.4 M.9 E.1 M.10 Y.5 E.2
    M.11 E.3 Y.6 E.4 E.5 H.4 TM.1 H.5 Y.7 H.6 H.7 GT.0 M.12 Y.8 M.13 Y.9 M.14 E.6 Y.10 M.15 E.7 Y.11 M.16
    E.8 Y.12 M.17 E.9 Y.13 E.10 Y.14 E.11 H.8 H.9 PV.0 TM.2 T1.0 H.10 Y.15 QKV.0 H.11 Y.16 TP.0 M.18 E.12
    Y.17 M.19 M.20 Y.18 M.21 E.13 Y.19 M.22 E.14 Y.20 E.15 M.23 E.16 Y.21 Y.22 E.17 TM.3 H.12 Y.23 H.13
    PV.1 H.14 H.15 Y.24 E.18 Y.25 TP.1 E.19 Y.26 E.20 E.21 Y.27 E.22 E.23 Y.28 PV.2 H.16 PV.3 TP.2 Y.29
    TP.3 H.17 Y.30 TO.0 Y.31 PJ.0 TK.0 TQ.0 Y.32 Y.33 Y.34 T2.0 Y.35 RL.0
"""

SCALAR_ORDER = """
    gelu.0 gelu.1 gelu.2 gelu.3 gelu.4 gelu.5 gelu.6 gelu.7 router.0 exp.0 exp.1 exp.2 exp.3 exp.4 exp.5
    gelu.8 gelu.9 gelu.10 gelu.11 gelu.12 gates.0 gelu.13 gelu.14 gelu.15 exp.6 exp.7 exp.8 exp.9 exp.10
    exp.11 gelu.16 gelu.17 gelu.18 gelu.19 xnT.0 out.0 v.0 gelu.20 gelu.21 gelu.22 gelu.23 exp.12 exp.13
    exp.14 exp.15 exp.16 exp.17 gelu.24 gelu.25 gelu.26 gelu.27 out.1 gelu.28 gelu.29 gelu.30 gelu.31
    exp.18 exp.19 exp.20 exp.21 exp.22 exp.23 out.2 gelu.32 gelu.33 out.3 gelu.34 gelu.35 heads.0 kst.0
    qst.0 x2T.0 x2h.0
"""

VECTOR_ORDER = """
    max.0 max.1 max.2 max.3 max.4 max.5 parts.0 turned.0 max.6 max.7 max.8 max.9 max.10 max.11 parts.1
    turned.1 route.0 add.0 max.12 max.13 max.14 add.1 max.15 max.16 max.17 parts.2 mean.0 add.2 norm.0
    turned.2 add.3 qk.0 divide.0 max.18 max.19 max.20 max.21 max.22 max.23 parts.3 add.4 turned.3 divide.1
    add.5 add.6 divide.2 divide.3 residual.0 mean2.0 norm2.0 add.7 x2l.0 add.8 logits.0
"""

POOL_ORDER = """
    mask.0 mask.1 mask.2 mask.3 mask.4 mask.5 mask.6 root.0 mask.7 mask.8 mask.9 mask.10 mask.11 mask.12
    mask.13 mask.14 mask.15 mask.16 mask.17 spreadk.0 spreadq.0 mask.18 mask.19 mask.20 mask.21 mask.22
    mask.23 root2.0 v.0
"""

FIRST_TENSOR_ORDER = """
    T1.0 M.0 M.1 QKV.0 M.2 M.3 M.4 M.5 M.6 TM.0 M.7 M.8 E.0 M.9 E.1 E.2 M.10 E.3 M.11 E.4 TM.1 M.12 E.5
    M.13 E.6 M.14 M.15 E.7 M.16 E.8 M.17 E.9 E.10 E.11 PV.0 TM.2 TP.0 M.18 E.12 M.19 M.20 M.21 M.22 M.23
    E.13 E.14 E.15 E.16 TM.3 E.17 E.18 PV.1 E.19 E.20 TP.1 E.21 E.22 E.23 PV.2 PV.3 TP.2 TP.3 TK.0 TO.0
    PJ.0 TQ.0 T2.0 RL.0
"""

FIRST_SCALAR_ORDER = """
    high.0 xnT.0 v.0 exp.0 exp.1 exp.2 exp.3 exp.4 high.1 exp.5 high.2 exp.6 exp.7 exp.8 exp.9 exp.10
    high.3 exp.11 out.0 exp.12 high.4 high.5 high.6 exp.13 exp.14 exp.15 exp.16 exp.17 high.7 high.8 out.1
    exp.18 exp.19 exp.20 exp.21 exp.22 exp.23 out.2 out.3 heads.0 kst.0 qst.0 x2T.0 x2h.0
"""

FIRST_VECTOR_ORDER = """
    mean.0 norm.0 max.0 max.1 qk.0 max.2 max.3 max.4 max.5 parts.0 max.6 turned.0 max.7 max.8 max.9 max.10
    max.11 parts.1 turned.1 max.12 max.13 max.14 max.15 max.16 max.17 parts.2 turned.2 divide.0 max.18
    max.19 max.20 max.21 max.22 max.23 parts.3 spreadk.0 turned.3 divide.1 spreadq.0 divide.2 divide.3
    residual.0 mean2.0 norm2.0 logits.0 x2l.0
"""

FIRST_POOL_ORDER = """
    root.0 mask.0 mask.1 mask.2 mask.3 mask.4 mask.5 mask.6 mask.7 mask.8 mask.9 mask.10 low.0 mask.11
    low.1 low.2 mask.12 mask.13 mask.14 mask.15 mask.16 mask.17 low.3 low.4 low.5 mask.18 mask.19 mask.20
    low.6 mask.21 mask.22 mask.23 low.7 root2.0 low.8 v.0
"""

PREPARATION = ("T1", "QKV", "TK", "TQ", "xnT", "v", "kst", "qst", "mean", "norm", "qk", "root", "spreadk", "spreadq")


def batch_steps(order, prepare=True):
    steps = [(kind, int(n)) for kind, n in (step.split(".") for step in order.split())]
    return [s for s in steps if prepare or s[0] not in PREPARATION]


def hidden_steps(e):
    return [("H", 2 * e), ("H", 2 * e + 1)]


def out_steps(e):
    return [("Y", NT * e + i) for i in range(NT)]


def expert_steps():
    steps = hidden_steps(0)
    for e in range(NE + 1):
        if e < NE:
            steps += hidden_steps(e + 1)
        if e == 2:
            steps.append(("GT", 0))
        steps += out_steps(e)
    return steps


PHASES = {"prologue": [("T1", 0), ("QKV", 0), ("B1", 0), ("TK", 0), ("TQ", 0)], "first": batch_steps(FIRST_TENSOR_ORDER),
          "second": batch_steps(TENSOR_ORDER), "loop": batch_steps(TENSOR_ORDER),
          "last": batch_steps(TENSOR_ORDER, False),
          "experts": expert_steps()}


def place_banks():
    places, at = {}, 0
    last = [None] * 5
    for phase, steps in PHASES.items():
        places[phase] = {}
        last = [(who, when - 1) for who, when in (x or (None, 0) for x in last)]
        for kind, n in steps:
            if kind == "Y":
                place = 3 + n // NT % 2
            elif kind in ("PV", "GT", "B1"):
                place = 3
            elif kind == "RL":
                place = 4
            else:
                place, at = at, (at + 1) % 3
            places[phase][kind, n] = place, *last[place]
            last[place] = ((kind, n), 0)
    assert {u: p[0] for u, p in places["second"].items()} == {u: p[0] for u, p in places["loop"].items()}
    return places


PLACES = place_banks()


def attn_moe_kernel(nc, x, wq, wk, wv, wo, dirs, scale, wfc_s, bfc_s, wproj_s, bproj_s, wr, wfc, bfc,
                    wproj, bproj, out):
    with ExitStack() as ctx:
        def sb(name, shape, dt=F32):
            return ctx.enter_context(nc.sbuf_tensor(name, shape, dt))

        def sem(name):
            return ctx.enter_context(nc.semaphore(name))

        ident = sb("ident", [P, P])
        identb = sb("identb", [P, P], BF16)
        future = sb("future", [P, P], BF16)
        iota = sb("iota", [P, NE])
        wqkv = sb("wqkv", [P, 2 * H * QD + C])
        dirs_all = sb("dirs_all", [P, H * QD])
        scale_all = sb("scale_all", [P, 1])
        fold = sb("fold", [P, H * QD])
        dots = sb("dots", [P, H])
        wo_sb = sb("wo_sb", [P, C])
        wr_sb = sb("wr_sb", [P, NE])
        w1 = sb("w1", [P, NE + 1, HID])
        w1h = sb("w1h", [P, NE + 1, HID], F32R)
        w1l = sb("w1l", [P, NE + 1, HID], F32R)
        w2 = sb("w2", [P, NE + 1, NQ, C])
        b1rows = sb("b1rows", [(NE + 1) * NQ, P])
        b1 = sb("b1", [P, (NE + 1) * NQ])
        b2 = sb("b2", [NE + 1, C])
        xin = sb("xin", [P, NT, C])
        xres = sb("xres", [P, NT, C])
        stats = sb("stats", [P, NT, 6])
        meanvar = sb("meanvar", [P, NT, 2])
        rstd = sb("rstd", [P, NT])
        var_eps = sb("var_eps", [P, NT])
        half = sb("half", [P, NT])
        xn = sb("xn", [P, NT, C])
        xnT = sb("xnT", [P, T])
        parts = sb("parts", [P, NPART, 2, NT, H * QD], BF16)
        rest = sb("rest", [P, 2, NT, H * QD])
        qrows = sb("qrows", [P, NT, H, W], BF16)
        krows = sb("krows", [P, NT, H, W], BF16)
        kst = sb("kst", [P, G, T], BF16)
        qst = sb("qst", [P, G, T], BF16)
        qmst = sb("qmst", [P, 2, T], BF16)
        kpad = sb("kpad", [P, G, R, T], BF16)
        vext = sb("vext", [P, NT, H, W])
        negmax = sb("negmax", [P, G, NT, R])
        mrest = sb("mrest", [P, NT, R])
        probs = sb("probs", [P, 2, R, PW])
        vstage = sb("vstage", [P, NT, C])
        ot = sb("ot", [P, 2, T])
        rsum = sb("rsum", [P, 2, NT, R])
        onorm = sb("onorm", [P, NT, C])
        onT = sb("onT", [P, T])
        x1 = sb("x1", [P, NT, C])
        x2n = sb("x2n", [P, NT, C])
        x2T = sb("x2T", [P, T])
        x2h = sb("x2h", [P, T], F32R)
        x2l = sb("x2l", [P, T], F32R)
        lneg = sb("lneg", [P, NT])
        lsh = sb("lsh", [P, NT, NE])
        pexp = sb("pexp", [P, NT, NE])
        psum_r = sb("psum_r", [P, NT])
        prcp = sb("prcp", [P, NT])
        pr = sb("pr", [P, NT, NE])
        top = sb("top", [P, NT, 8])
        topi = sb("topi", [P, NT, 8], U32)
        topf = sb("topf", [P, NT, 2])
        wsum = sb("wsum", [P, NT])
        wrcp = sb("wrcp", [P, NT])
        wtop = sb("wtop", [P, NT, 2])
        hot = sb("hot", [P, 2, NT, NE])
        gate = sb("gate", [P, NT, NE + 1])
        gateT = sb("gateT", [NE + 1, T])
        hidden = w1[:, 0:2 * NQ, :].rearrange("p (a q) t -> p a q t", a=2)
        acc = sb("acc", [P, NT, C])
        y = sb("y", [P, NT, C])

        banks = ctx.enter_context(nc.psum_tensor("banks", [P, 8, 512], F32))

        x_loaded, xres_loaded, proj_loaded = sem("x_loaded"), sem("xres_loaded"), sem("proj_loaded")
        kpad_loaded, out_stored = sem("kpad_loaded"), sem("out_stored")
        b1_loaded, w1_loaded, w2_loaded = sem("b1_loaded"), sem("w1_loaded"), sem("w2_loaded")
        pool_made = sem("pool_made")
        eyes_made, consts_made, kpad_zeroed = sem("eyes_made"), sem("consts_made"), sem("kpad_zeroed")
        w1_high, w1_split = sem("w1_high"), sem("w1_split")
        proj_folded = sem("proj_folded")
        b1_turned, b1_ready = sem("b1_turned"), sem("b1_ready")
        var_ready, rstd_ready = sem("var_ready"), sem("rstd_ready")
        dve_step = sem("dve_step")
        ln1_done, xn_turned, xnT_ready = sem("ln1_done"), sem("xn_turned"), sem("xnT_ready")
        qkv_done, v_staged, v_ready, qkv_free, parts_ready = sem("qkv_done"), sem("v_staged"), sem("v_ready"), sem("qkv_free"), sem("parts_ready")
        k_spread, q_spread = sem("k_spread"), sem("q_spread")
        k_turned, q_turned, kst_ready, qst_ready = sem("k_turned"), sem("q_turned"), sem("kst_ready"), sem("qst_ready")
        m_scores, m_taken, m_parts = sem("m_scores"), sem("m_taken"), sem("m_parts")
        qm_turned, qmst_ready = sem("qm_turned"), sem("qmst_ready")
        scores_ready, exp_done, masked = sem("scores_ready"), sem("exp_done"), sem("masked")
        pv_done, ot_ready, ot_turned, onorm_ready = sem("pv_done"), sem("ot_ready"), sem("ot_turned"), sem("onorm_ready")
        on_turned, onT_ready, proj_done, x1_ready = sem("on_turned"), sem("onT_ready"), sem("proj_done"), sem("x1_ready")
        ln2_done, x2_turned, x2_high, x2T_ready, x2_split = sem("ln2_done"), sem("x2_turned"), sem("x2_high"), sem("x2T_ready"), sem("x2_split")
        logits_done, logits_taken, pexp_ready = sem("logits_done"), sem("logits_taken"), sem("pexp_ready")
        gates_ready, gate_turned, gateT_ready = sem("gates_ready"), sem("gate_turned"), sem("gateT_ready")
        h_ready, gelu_done, y_done, y_taken, out_ready = sem("h_ready"), sem("gelu_done"), sem("y_done"), sem("y_taken"), sem("out_ready")

        PROJ_LOADS, W1_LOADS, W2_LOADS = 6, 2, 5

        def ring(slot):
            return banks[:, 2 * slot:2 * slot + 2, :]

        def flat(slot):
            return ring(slot).rearrange("p a c -> p (a c)")

        def one_bank(place):
            return banks[:, 2 * place if place < 3 else 3 + place, :]

        def unit_view(slot, tiles):
            if tiles >= 3:
                return ring(slot)[:, :, 0:P * tiles]
            if tiles == 2:
                return flat(slot).rearrange("p (n w) -> p n w", w=2 * P)
            return banks[:, 2 * slot, :].rearrange("p (n w) -> p n w", w=P)

        def opens_bank(tiles, n):
            return tiles >= 3 or (tiles == 2 and n % 2 == 0) or n == 0

        def six(cols=512):
            return banks[:, 6, 0:cols]

        def seven(cols=512):
            return banks[:, 7, 0:cols]

        def y_bank(e):
            return banks[:, 6 + e % 2, :].rearrange("p (i c) -> p i c", i=NT)

        def wait_earlier(eng, semaphore, value):
            if not isinstance(value, int) or value > 0:
                eng.wait_ge(semaphore, value)

        def wait_apart(eng, semaphore, value):
            eng.wait_ge(consts_made, 1)
            eng.wait_ge(semaphore, value)

        def batch_loop(eng, body):
            body(0, "first", False, True)
            body(1, "second", True, True)
            with eng.Fori(2, B - 1) as b:
                body(b, "loop", True, True)
            body(B - 1, "last", True, False)

        def part(n, which):
            v = parts[:, n, which].rearrange("p i (h d) -> p (i h) d", d=QD)
            return v.unsqueeze(2).to_broadcast([P, NT * H, NPART, QD])

        def spread_k_parts(eng):
            kv = krows[:].rearrange("p i h s -> p (i h) s")
            for c in range(NPART):
                dst = kv[:, :, SLOT0:SLOT0 + 27].rearrange("p h (a c d) -> p h a c d", a=NPART, c=NPART)[:, :, :, c, :]
                last = eng.tensor_copy(dst, part(c, 1))
            last.then_inc(k_spread, 1)

        def spread_q_parts(eng):
            qv = qrows[:].rearrange("p i h s -> p (i h) s")
            for a in range(NPART):
                dst = qv[:, :, SLOT0 + 9 * a:SLOT0 + 9 * a + 9].rearrange("p h (c d) -> p h c d", c=NPART)
                last = eng.tensor_copy(dst, part(a, 0))
            last.then_inc(q_spread, 1)

        block = ctx.enter_context(nc.Block())

        @block.sync
        def _(sp):
            xv = x.rearrange("b (i p) c -> p (b i) c", p=P)
            ov = out.rearrange("b (i p) c -> p (b i) c", p=P)
            sp.dma_start(xin[:], xv[:, 0:NT, :]).then_inc(x_loaded, 16)
            sp.dma_start(wqkv[:, 0:48], wq).then_inc(proj_loaded, 16)
            sp.dma_start(wqkv[:, 48:96], wk).then_inc(proj_loaded, 16)
            sp.dma_start(wqkv[:, 96:224], wv).then_inc(proj_loaded, 16)
            sp.dma_start(dirs_all[:], dirs.rearrange("(o h) d -> o (h d)", o=1).partition_broadcast(P)).then_inc(proj_loaded, 16)
            sp.dma_start(scale_all[:], scale.rearrange("(o h) -> o h", o=1).partition_broadcast(P)).then_inc(proj_loaded, 16)
            sp.dma_start(wo_sb[:], wo).then_inc(proj_loaded, 16)
            sp.dma_start(b1rows[0:NE * NQ, :], bfc.rearrange("e (q p) -> (e q) p", p=P)).then_inc(b1_loaded, 16)
            sp.dma_start(b1rows[NE * NQ:(NE + 1) * NQ, :], bfc_s.rearrange("(q p) -> q p", p=P)).then_inc(b1_loaded, 16)
            sp.wait_ge(ln1_done, 1)
            sp.dma_start(xin[:], xv[:, NT:2 * NT, :]).then_inc(x_loaded, 16)
            sp.dma_start(w1[:, 0:NE, :], wfc.rearrange("e c h -> c e h")).then_inc(w1_loaded, 16)
            sp.dma_start(w1[:, NE, :], wfc_s).then_inc(w1_loaded, 16)

            def spread_k(bb):
                wait_apart(sp, kst_ready, bb + 1)
                for r in range(R):
                    sp.dma_start(kpad[W * r:W * r + W, :, r, :], kst[W * r:W * r + W, :, :]).then_inc(kpad_loaded, 16)

            def store(f):
                sp.dma_start(ov[:, bass.ds(f * NT, NT), :], y[:]).then_inc(out_stored, 16)

            def body(b, phase, experts, prepare):
                if prepare and experts:
                    wait_apart(sp, ln1_done, b + 1)
                    sp.dma_start(xin[:], xv[:, bass.ds(b * NT + NT, NT), :]).then_inc(x_loaded, 16)
                if experts:
                    wait_apart(sp, x1_ready, b)
                sp.dma_start(xres[:], xv[:, bass.ds(b * NT, NT), :]).then_inc(xres_loaded, 16)
                if prepare:
                    spread_k(b + 1)
                if experts:
                    wait_apart(sp, out_ready, b)
                    store(b - 1)

            sp.wait_ge(kpad_zeroed, 1)
            spread_k(0)
            sp.dma_start(w2[:, 0:NE].rearrange("p e q n -> p (e q) n"), wproj.rearrange("e (q p) n -> p (e q) n", p=P)).then_inc(w2_loaded, 16)
            sp.dma_start(w2[:, NE], wproj_s.rearrange("(q p) n -> p q n", p=P)).then_inc(w2_loaded, 16)
            sp.dma_start(b2[0:NE, :], bproj).then_inc(w2_loaded, 16)
            sp.dma_start(b2[NE:NE + 1, :], bproj_s.rearrange("(o n) -> o n", o=1)).then_inc(w2_loaded, 16)
            sp.dma_start(wr_sb[:], wr).then_inc(w2_loaded, 16)
            batch_loop(sp, body)
            sp.wait_ge(out_ready, B)
            store(B - 1)
            sp.wait_ge(out_stored, 16 * B)

        @block.gpsimd
        def _(pool):
            made = 0
            unit_seen = pool.alloc_register("unit_seen")
            batch_seen = pool.alloc_register("batch_seen")
            group_seen = pool.alloc_register("group_seen")
            batch_next = pool.alloc_register("batch_next")
            for counter in (unit_seen, batch_seen, group_seen):
                pool.reg_mov(counter, 0)
            pool.reg_mov(batch_next, 1)

            def link(ins):
                nonlocal made
                made += 1
                ins.then_inc(pool_made, 1)
                pool.wait_ge(pool_made, made)

            def root(nth):
                pool.wait_ge(var_ready, nth)
                pool.tensor_tensor(rstd[:], var_eps[:], half[:], ALU.pow).then_inc(rstd_ready, 1)

            pool.memset(half[:], -0.5)
            pool.memset(ident[:], 0.0)
            link(pool.memset(identb[:], 0.0))
            for m in (ident, identb):
                last = pool.affine_select(out=m[:], in_=m[:], compare_op=ALU.not_equal, fill=1.0, base=0,
                                          pattern=[[-1, P]], channel_multiplier=1)
            last.then_inc(eyes_made, 1)
            root(1)
            link(pool.memset(future[:], 0.0))
            pool.affine_select(out=future[:], in_=future[:], compare_op=ALU.is_ge, fill=NEG, base=0,
                               pattern=[[-1, P]], channel_multiplier=1)
            link(pool.memset(vext[:], 0.0))
            pool.memset(vext[:, :, :, HD:HD + 1], 1.0)
            pool.memset(gate[:], 1.0).then_inc(consts_made, 1)

            def place_values():
                pool.wait_ge(consts_made, 1)
                pool.wait_ge(v_staged, batch_next)
                pool.wait_ge(pv_done, group_seen)
                pool.tensor_copy(vext[:, :, :, 0:HD], vstage[:].rearrange("p i (h d) -> p i h d", d=HD)).then_inc(v_ready, 1)

            def mask_probs(b, n):
                g, (tiles, heads) = n // NU, UNITS[n % NU]
                pool.reg_add(unit_seen, unit_seen, 1)
                pool.wait_ge(consts_made, 1)
                pool.wait_ge(exp_done, unit_seen)
                v = probs[:, g % 2, heads[0]:heads[-1] + 1, PCOL[tiles]:PCOL[tiles] + P]
                pool.affine_select(out=v, in_=v, compare_op=ALU.is_ge, fill=0.0, base=0,
                                   pattern=[[0, len(heads)], [1, P]], channel_multiplier=-1).then_inc(masked, 1)

            def split_low(e):
                pool.wait_ge(w1_high, e + 1)
                pool.tensor_tensor(w1l[:, e, :], w1[:, e, :], w1h[:, e, :].bitcast(F32), ALU.subtract).then_inc(w1_split, 1)

            def body(b, phase, experts, prepare):
                pool.reg_add(batch_seen, batch_seen, 1)
                pool.reg_add(batch_next, batch_next, 1)
                pool.reg_add(group_seen, group_seen, G)
                for kind, n in batch_steps(POOL_ORDER if experts else FIRST_POOL_ORDER, prepare):
                    if kind == "mask":
                        mask_probs(b, n)
                    elif kind == "low":
                        split_low(n)
                    elif kind == "root":
                        root(2 * b + 2)
                    elif kind == "root2":
                        root(2 * b + (3 if prepare else 2))
                    elif kind == "spreadk":
                        pool.wait_ge(consts_made, 1)
                        pool.wait_ge(parts_ready, batch_next)
                        pool.wait_ge(k_turned, batch_seen)
                        spread_k_parts(pool)
                    elif kind == "spreadq":
                        pool.wait_ge(consts_made, 1)
                        pool.wait_ge(qm_turned, group_seen)
                        pool.memset(qrows[:, :, :, 0:NPART], 0.0)
                        spread_q_parts(pool)
                    elif kind == "v":
                        place_values()

            pool.wait_ge(v_staged, 1)
            pool.tensor_copy(vext[:, :, :, 0:HD], vstage[:].rearrange("p i (h d) -> p i h d", d=HD)).then_inc(v_ready, 1)
            batch_loop(pool, body)

        @block.scalar
        def _(act):
            def copy(dst, src):
                return nc.scalar.activation(dst, src, ACT.Copy)

            def evacuate_xn(bb, place):
                act.wait_ge(xn_turned, bb + 1)
                wait_earlier(act, qkv_done, bb)
                copy(xnT[:], flat(place)[:, 0:T]).then_inc(xnT_ready, 1)

            def stage_v(bb, place):
                act.wait_ge(qkv_done, bb + 1)
                wait_earlier(act, v_ready, bb)
                src = flat(place).rearrange("p (i c) -> p i c", i=NT)[:, :, 96:224]
                copy(vstage[:], src).then_inc(v_staged, 1)

            def evacuate_k(bb, place):
                act.wait_ge(k_turned, bb + 1)
                wait_earlier(act, kpad_loaded, bb * 16 * R)
                copy(kst[:].rearrange("p g t -> p (g t)"), flat(place).bitcast(BF16)).then_inc(kst_ready, 1)

            def evacuate_q(bb, place):
                act.wait_ge(q_turned, bb + 1)
                wait_earlier(act, m_scores, bb * M_PER)
                copy(qst[:].rearrange("p g t -> p (g t)"), flat(place).bitcast(BF16)).then_inc(qst_ready, 1)

            def exps(b, n, at):
                g, (tiles, heads) = n // NU, UNITS[n % NU]
                act.wait_ge(scores_ready, b * E_PER + n + 1)
                wait_earlier(act, pv_done, b * G + max(0, g - 1))
                nc.scalar.activation(probs[:, g % 2, heads[0]:heads[-1] + 1, PCOL[tiles]:PCOL[tiles] + P * tiles],
                                     unit_view(at["E", n][0], tiles), ACT.Exp).then_inc(exp_done, 1)

            def evacuate_o(b, g):
                act.wait_ge(pv_done, b * G + g + 1)
                wait_earlier(act, ot_turned, b * G + max(0, g - 1))
                copy(ot[:, g % 2, :], six()).then_inc(ot_ready, 1)

            def gelu(f, n, at):
                e, q = n // NQ, n % NQ
                if q % 2 == 0:
                    act.wait_ge(h_ready, f * 2 * (NE + 1) + 2 * e + q // 2 + 1)
                if q == 0:
                    wait_earlier(act, y_done, f * Y_PER + max(0, e - 1))
                nc.scalar.activation(hidden[:, e % 2, q, :], ring(at["H", 2 * e + q // 2][0])[:, q % 2, :],
                                     ACT.Gelu_apprx_tanh, bias=b1[:, e * NQ + q:e * NQ + q + 1]).then_inc(gelu_done, 1)

            def exp_logits(f):
                act.wait_ge(logits_taken, f + 1)
                nc.scalar.activation(pexp[:], lsh[:], ACT.Exp).then_inc(pexp_ready, 1)

            def evacuate_gates(f):
                act.wait_ge(gate_turned, f + 1)
                copy(gateT[:], six()[0:NE + 1, :]).then_inc(gateT_ready, 1)

            def split_high(e):
                act.wait_ge(w1_loaded, 16 * W1_LOADS)
                copy(w1h[:, e, :], w1[:, e, :]).then_inc(w1_high, 1)

            def body(b, phase, experts, prepare):
                at = PLACES[phase]
                for kind, n in batch_steps(SCALAR_ORDER if experts else FIRST_SCALAR_ORDER, prepare):
                    if kind == "gelu":
                        gelu(b - 1, n, at)
                    elif kind == "exp":
                        exps(b, n, at)
                    elif kind == "high":
                        split_high(n)
                    elif kind == "router":
                        exp_logits(b - 1)
                    elif kind == "out":
                        evacuate_o(b, n)
                    elif kind == "gates":
                        evacuate_gates(b - 1)
                    elif kind == "heads":
                        act.wait_ge(on_turned, b + 1)
                        copy(onT[:], flat(at["TO", 0][0])[:, 0:T]).then_inc(onT_ready, 1)
                    elif kind == "x2T":
                        act.wait_ge(x2_turned, b + 1)
                        copy(x2T[:], flat(at["T2", 0][0])[:, 0:T]).then_inc(x2T_ready, 1)
                    elif kind == "x2h":
                        copy(x2h[:], flat(at["T2", 0][0])[:, 0:T]).then_inc(x2_high, 1)
                    elif kind == "xnT":
                        evacuate_xn(b + 1, at["T1", 0][0])
                    elif kind == "v":
                        stage_v(b + 1, at["QKV", 0][0])
                    elif kind == "kst":
                        evacuate_k(b + 1, at["TK", 0][0])
                    elif kind == "qst":
                        evacuate_q(b + 1, at["TQ", 0][0])

            at = PLACES["prologue"]
            evacuate_xn(0, at["T1", 0][0])
            stage_v(0, at["QKV", 0][0])
            evacuate_k(0, at["TK", 0][0])
            evacuate_q(0, at["TQ", 0][0])
            act.wait_ge(b1_ready, 1)
            batch_loop(act, body)
            exp_logits(B - 1)
            for e in range(NE + 1):
                for q in range(NQ):
                    gelu(B - 1, NQ * e + q, PLACES["experts"])
                if e == 3:
                    evacuate_gates(B - 1)

        @block.vector
        def _(dve):
            class Chain:

                def __init__(self):
                    dve.sem_clear(dve_step)
                    self.n = 0

                def __call__(self, ins):
                    self.n += 1
                    ins.then_inc(dve_step, 1)
                    dve.wait_ge(dve_step, self.n)

            def bc(ap, n):
                shape = list(ap.shape) + [n]
                return ap.unsqueeze(len(ap.shape)).to_broadcast(shape)

            def mean_variance(link, src):
                for i in range(NT):
                    last = dve.bn_stats(stats[:, i, :], src[:, i, :])
                link(last)
                for i in range(NT):
                    last = dve.bn_aggr(meanvar[:, i, :], stats[:, i, :])
                link(last)
                dve.tensor_scalar(var_eps[:], meanvar[:, :, 1], EPS, None, ALU.add).then_inc(var_ready, 1)

            def normalized(dst, src, nth):
                dve.wait_ge(rstd_ready, nth)
                for i in range(NT):
                    last = dve.tensor_scalar(dst[:, i, :], src[:, i, :], meanvar[:, i, 0:1], rstd[:, i:i + 1],
                                             ALU.subtract, ALU.mult)
                return last

            def first_mean(bb, link):
                dve.wait_ge(x_loaded, bb * 16 + 16)
                mean_variance(link, xin)

            def first_norm(bb, nth):
                wait_earlier(dve, xn_turned, bb)
                normalized(xn, xin, nth).then_inc(ln1_done, 1)

            def split_qk(bb, link, place):
                dve.wait_ge(v_staged, bb + 1)
                wait_earlier(dve, q_spread, bb)
                qk = flat(place).rearrange("p (i c) -> p i c", i=NT)[:, :, 0:96].rearrange("p i (w c) -> p w i c", w=2)
                link(dve.tensor_copy(parts[:, 0], qk))
                dve.tensor_tensor(rest[:], qk, parts[:, 0], ALU.subtract).then_inc(qkv_free, 1)
                dve.wait_ge(qkv_free, bb + 1)
                link(dve.tensor_copy(parts[:, 1], rest[:]))
                dve.tensor_tensor(parts[:, 2], rest[:], parts[:, 1], ALU.subtract).then_inc(parts_ready, 1)

            def take_maxima(b, n, at):
                g, (tiles, heads) = n // NU, UNITS[n % NU]
                dve.wait_ge(m_scores, b * M_PER + n + 1)
                dve.tensor_reduce(negmax[:, g, tiles - 1, heads[0]:heads[-1] + 1], unit_view(at["M", n][0], tiles),
                                  AX.X, ALU.max, negate=True).then_inc(m_taken, 1)

            def split_maxima(b, g, link):
                dve.wait_ge(m_taken, b * M_PER + g * NU + NU)
                dst = qrows[:, :, R * g:R * g + R, :]
                link(dve.tensor_copy(dst[:, :, :, 0], negmax[:, g]))
                link(dve.tensor_tensor(mrest[:], negmax[:, g], dst[:, :, :, 0], ALU.subtract))
                link(dve.tensor_copy(dst[:, :, :, 1], mrest[:]))
                dve.tensor_tensor(dst[:, :, :, 2], mrest[:], dst[:, :, :, 1], ALU.subtract).then_inc(m_parts, 1)

            def evacuate_qm(b, g, place):
                dve.wait_ge(qm_turned, b * G + g + 1)
                wait_earlier(dve, scores_ready, b * E_PER + NU * max(0, g - 1))
                dve.tensor_copy(qmst[:, g % 2, :], one_bank(place)[:, 0:T // 2].bitcast(BF16)).then_inc(qmst_ready, 1)

            def normalize(b, g, link, place):
                dve.wait_ge(ot_turned, b * G + g + 1)
                src = one_bank(place).rearrange("p (i r w) -> p i r w", i=NT, r=R)
                link(dve.reciprocal(rsum[:, g % 2], src[:, :, :, HD]))
                dst = onorm[:].rearrange("p i (g r d) -> p i g r d", g=G, r=R)[:, :, g]
                dve.tensor_tensor(dst, src[:, :, :, 0:HD], bc(rsum[:, g % 2], HD), ALU.mult).then_inc(onorm_ready, 1)

            def shift_logits(b, link):
                dve.wait_ge(logits_done, b + 1)
                logits = seven(NT * NE).rearrange("p (i e) -> p i e", i=NT)
                link(dve.tensor_reduce(lneg[:], logits, AX.X, ALU.max, negate=True))
                dve.tensor_tensor(lsh[:], logits, bc(lneg[:], NE), ALU.add).then_inc(logits_taken, 1)

            def route(f, link):
                dve.wait_ge(pexp_ready, f + 1)
                link(dve.tensor_reduce(psum_r[:], pexp[:], AX.X, ALU.add))
                link(dve.reciprocal(prcp[:], psum_r[:]))
                link(dve.tensor_tensor(pr[:], pexp[:], bc(prcp[:], NE), ALU.mult))
                for i in range(NT):
                    last = dve.max(top[:, i, :], pr[:, i, :])
                link(last)
                for i in range(NT):
                    last = dve.max_index(topi[:, i, :], top[:, i, :], pr[:, i, :])
                dve.tensor_tensor(wsum[:], top[:, :, 0], top[:, :, 1], ALU.add)
                link(last)
                link(dve.tensor_copy(topf[:], topi[:, :, 0:2]))
                link(dve.reciprocal(wrcp[:], wsum[:]))
                link(dve.tensor_tensor(wtop[:], top[:, :, 0:2], bc(wrcp[:], 2), ALU.mult))
                every = iota[:].unsqueeze(1).to_broadcast([P, NT, NE])
                for n in range(2):
                    last = dve.tensor_tensor(hot[:, n], every, bc(topf[:, :, n], NE), ALU.is_equal)
                link(last)
                for n in range(2):
                    last = dve.tensor_tensor(hot[:, n], hot[:, n], bc(wtop[:, :, n], NE), ALU.mult)
                link(last)
                dve.tensor_tensor(gate[:, :, 0:NE], hot[:, 0], hot[:, 1], ALU.add).then_inc(gates_ready, 1)

            def add_expert(f, e):
                dve.wait_ge(y_done, f * Y_PER + e + 1)
                src = y_bank(e)
                if e == NE:
                    dve.wait_ge(y_taken, f * NE + e)
                    wait_earlier(dve, out_stored, f * 16)
                    dve.tensor_tensor(y[:], src, acc[:], ALU.add).then_inc(out_ready, 1)
                    return
                dve.wait_ge(gates_ready, f + 1)
                if e > 0:
                    dve.wait_ge(y_taken, f * NE + e)
                for i in range(NT):
                    last = dve.scalar_tensor_tensor(acc[:, i, :], src[:, i, :], gate[:, i, e:e + 1],
                                                    (acc if e else x1)[:, i, :], ALU.mult, ALU.add)
                last.then_inc(y_taken, 1)

            def residual(b, place):
                dve.wait_ge(proj_done, b + 1)
                dve.wait_ge(xres_loaded, b * 16 + 16)
                dve.tensor_tensor(x1[:], one_bank(place).rearrange("p (i c) -> p i c", i=NT), xres[:], ALU.add).then_inc(x1_ready, 1)

            def body(b, phase, experts, prepare):
                at = PLACES[phase]
                link = Chain()
                for kind, n in batch_steps(VECTOR_ORDER if experts else FIRST_VECTOR_ORDER, prepare):
                    if kind == "max":
                        take_maxima(b, n, at)
                    elif kind == "parts":
                        split_maxima(b, n, link)
                    elif kind == "turned":
                        evacuate_qm(b, n, at["TM", n][0])
                    elif kind == "divide":
                        normalize(b, n, link, at["TP", n][0])
                    elif kind == "add":
                        add_expert(b - 1, n)
                    elif kind == "route":
                        route(b - 1, link)
                    elif kind == "residual":
                        residual(b, at["PJ", 0][0])
                    elif kind == "mean2":
                        dve.wait_ge(x1_ready, b + 1)
                        mean_variance(link, x1)
                    elif kind == "norm2":
                        normalized(x2n, x1, 2 * b + (3 if prepare else 2)).then_inc(ln2_done, 1)
                    elif kind == "x2l":
                        dve.wait_ge(x2_high, b + 1)
                        dve.wait_ge(x2T_ready, b + 1)
                        dve.tensor_tensor(x2l[:], x2T[:], x2h[:].bitcast(F32), ALU.subtract).then_inc(x2_split, 1)
                    elif kind == "logits":
                        shift_logits(b, link)
                    elif kind == "mean":
                        first_mean(b + 1, link)
                    elif kind == "norm":
                        first_norm(b + 1, 2 * b + 2)
                    elif kind == "qk":
                        split_qk(b + 1, link, at["QKV", 0][0])
                    elif kind == "spreadk":
                        dve.wait_ge(parts_ready, b + 2)
                        dve.wait_ge(k_turned, b + 1)
                        spread_k_parts(dve)
                    elif kind == "spreadq":
                        dve.wait_ge(qm_turned, b * G + G)
                        dve.memset(qrows[:, :, :, 0:NPART], 0.0)
                        spread_q_parts(dve)

            link = Chain()
            dve.memset(qrows[:], 0.0)
            link(dve.memset(krows[:], 0.0))
            dve.memset(krows[:, :, :, 0:NPART], 1.0)
            first_mean(0, link)
            first_norm(0, 1)
            dve.wait_ge(proj_loaded, 16 * PROJ_LOADS)
            wk3 = wqkv[:, 48:96]
            link(dve.tensor_tensor(fold[:], wk3, dirs_all[:], ALU.mult))
            link(dve.tensor_reduce(dots[:], fold[:].rearrange("p (h d) -> p h d", d=QD), AX.X, ALU.add))
            link(dve.tensor_tensor(fold[:].rearrange("p (h d) -> p h d", d=QD), dirs_all[:].rearrange("p (h d) -> p h d", d=QD),
                                   bc(dots[:], QD), ALU.mult))
            dve.scalar_tensor_tensor(wk3, wk3, scale_all[:, 0:1], fold[:], ALU.mult, ALU.add).then_inc(proj_folded, 1)
            for e in range(NE):
                dve.memset(iota[:, e:e + 1], float(e))
            dve.memset(kpad[:].rearrange("p g r t -> p (g r t)").bitcast(F32), 0.0).then_inc(kpad_zeroed, 1)
            split_qk(0, link, PLACES["prologue"]["QKV", 0][0])
            dve.wait_ge(parts_ready, 1)
            spread_k_parts(dve)
            spread_q_parts(dve)
            dve.wait_ge(b1_turned, 1)
            dve.tensor_copy(b1[:], six((NE + 1) * NQ)).then_inc(b1_ready, 1)
            batch_loop(dve, body)
            route(B - 1, Chain())
            for e in range(NE + 1):
                add_expert(B - 1, e)

        @block.tensor
        def _(pe):
            mm = nc.tensor.matmul

            def turn(dst, src, eye):
                return nc.tensor.transpose(dst, src, eye)

            def turn_xn(bb, place):
                pe.wait_ge(ln1_done, bb + 1)
                for i in range(NT):
                    last = turn(flat(place)[:, P * i:P * i + P], xn[:, i, :], ident[:])
                last.then_inc(xn_turned, 1)

            def project(bb, place):
                if isinstance(bb, int) and bb == 0:
                    pe.wait_ge(proj_folded, 1)
                pe.wait_ge(xnT_ready, bb + 1)
                for i in range(NT):
                    last = mm(flat(place)[:, 2 * P * i:2 * P * i + 224], xnT[:, P * i:P * i + P], wqkv[:], start=True, stop=True)
                last.then_inc(qkv_done, 1)

            def turn_stacks(bb, place, rows, spread, turned):
                pe.wait_ge(spread, bb + 1)
                dst = flat(place).bitcast(BF16)
                for g in range(G):
                    for i in range(NT):
                        last = turn(dst[:, T * g + P * i:T * g + P * i + P],
                                    rows[:, i, R * g:R * g + R, :].rearrange("p h s -> p (h s)"), identb[:])
                last.then_inc(turned, 1)

            def max_scores(b, n, place):
                g, (tiles, heads) = n // NU, UNITS[n % NU]
                if n == 0:
                    pe.wait_ge(kpad_loaded, b * 16 * R + 16 * R)
                    pe.wait_ge(qst_ready, b + 1)
                dst, i = unit_view(place, tiles), tiles - 1
                for m, r in enumerate(heads):
                    mm(dst[:, m, :], qst[:, g, P * i:P * i + P], kpad[:, g, r, 0:P * tiles],
                       start=opens_bank(tiles, m), stop=False, skip_group_check=True)
                    last = mm(dst[:, m, P * i:P * i + P], identb[:], future[:], start=False, stop=True,
                              skip_group_check=True)
                last.then_inc(m_scores, 1)

            def scores(b, n, place):
                g, (tiles, heads) = n // NU, UNITS[n % NU]
                if n % NU == 0:
                    pe.wait_ge(qmst_ready, b * G + g + 1)
                dst, j = unit_view(place, tiles), NT - tiles
                for m, r in enumerate(heads):
                    last = mm(dst[:, m, :], kpad[:, g, r, P * j:P * j + P], qmst[:, g % 2, P * j:T],
                              start=opens_bank(tiles, m), stop=True, skip_group_check=True)
                last.then_inc(scores_ready, 1)

            def turn_maxima(b, g, place):
                pe.wait_ge(m_parts, b * G + g + 1)
                dst = one_bank(place)[:, 0:T // 2].bitcast(BF16)
                for i in range(NT):
                    last = turn(dst[:, P * i:P * i + P], qrows[:, i, R * g:R * g + R, :].rearrange("p h s -> p (h s)"),
                                identb[:])
                last.then_inc(qm_turned, 1)

            def values(b, g):
                pe.wait_ge(masked, b * E_PER + g * NU + NU)
                if g == 0:
                    pe.wait_ge(v_ready, b + 1)
                for j in range(NT):
                    tiles = NT - j
                    for r in range(R):
                        last = mm(banks[W * r:W * r + W, 6, P * j:T], vext[:, j, R * g + r, :],
                                  probs[:, g % 2, r, PCOL[tiles]:PCOL[tiles] + P * tiles], start=(j == 0), stop=(j == NT - 1))
                last.then_inc(pv_done, 1)

            def turn_values(b, g, place):
                pe.wait_ge(ot_ready, b * G + g + 1)
                for i in range(NT):
                    last = turn(one_bank(place)[:, P * i:P * i + P], ot[:, g % 2, P * i:P * i + P], ident[:])
                last.then_inc(ot_turned, 1)

            def turn_heads(b, place):
                pe.wait_ge(onorm_ready, b * G + G)
                for i in range(NT):
                    last = turn(flat(place)[:, P * i:P * i + P], onorm[:, i, :], ident[:])
                last.then_inc(on_turned, 1)

            def project_out(b, place):
                pe.wait_ge(onT_ready, b + 1)
                for i in range(NT):
                    last = mm(flat(place)[:, P * i:P * i + P], onT[:, P * i:P * i + P], wo_sb[:], start=True, stop=True)
                last.then_inc(proj_done, 1)

            def turn_x2(b, place):
                pe.wait_ge(ln2_done, b + 1)
                for i in range(NT):
                    last = turn(flat(place)[:, P * i:P * i + P], x2n[:, i, :], ident[:])
                last.then_inc(x2_turned, 1)

            def logits(b):
                if isinstance(b, int) and b == 0:
                    pe.wait_ge(w2_loaded, 16 * W2_LOADS)
                pe.wait_ge(x2T_ready, b + 1)
                for i in range(NT):
                    last = mm(seven()[:, NE * i:NE * i + NE], x2T[:, P * i:P * i + P], wr_sb[:], start=True, stop=True)
                last.then_inc(logits_done, 1)

            def first_layer(f, n, place):
                e, u = n // 2, n % 2
                if n == 0:
                    pe.wait_ge(x2_split, f + 1)
                for q in (2 * u, 2 * u + 1):
                    dst = ring(place)[:, q % 2, :]
                    wh, wl = w1h[:, e, P * q:P * q + P], w1l[:, e, P * q:P * q + P]
                    mm(dst, wh, x2h[:], start=True, stop=False)
                    mm(dst, wh, x2l[:], start=False, stop=False)
                    last = mm(dst, wl, x2h[:], start=False, stop=True)
                last.then_inc(h_ready, 1)

            def second_layer(f, n):
                e, i = n // NT, n % NT
                if i == 0:
                    pe.wait_ge(gelu_done, f * GELU_PER + NQ * e + NQ)
                for q in range(NQ):
                    last = mm(y_bank(e)[:, i, :], hidden[:, e % 2, q, P * i:P * i + P], w2[:, e, q, :],
                              start=(q == 0), stop=(q == NQ - 1 and e < NE))
                if e == NE:
                    if i == 0:
                        pe.wait_ge(gateT_ready, f + 1)
                    last = mm(y_bank(e)[:, i, :], gateT[:, P * i:P * i + P], b2[:], start=False, stop=True)
                if i == NT - 1:
                    last.then_inc(y_done, 1)

            def turn_gates(f):
                pe.wait_ge(gates_ready, f + 1)
                for i in range(NT):
                    last = turn(six()[0:NE + 1, P * i:P * i + P], gate[:, i, :], ident[:])
                last.then_inc(gate_turned, 1)

            def turn_biases():
                pe.wait_ge(b1_loaded, 32)
                n = (NE + 1) * NQ
                turn(six(n), b1rows[:], ident[0:n, 0:n]).then_inc(b1_turned, 1)

            def wait_read(b, unit, when):
                if unit is None:
                    return
                kind, n = unit
                a, f, bb = b + when, b - 1 + when, b + 1 + when
                if kind == "M":
                    pe.wait_ge(m_taken, a * M_PER + n + 1)
                elif kind == "E":
                    pe.wait_ge(exp_done, a * E_PER + n + 1)
                elif kind == "TO":
                    pe.wait_ge(onT_ready, a + 1)
                elif kind == "T2":
                    pe.wait_ge(x2_high, a + 1)
                elif kind == "TM":
                    pe.wait_ge(qmst_ready, a * G + n + 1)
                elif kind == "PV":
                    pe.wait_ge(ot_ready, a * G + n + 1)
                elif kind == "TP":
                    pe.wait_ge(onorm_ready, a * G + n + 1)
                elif kind == "PJ":
                    pe.wait_ge(x1_ready, a + 1)
                elif kind == "RL":
                    pe.wait_ge(logits_taken, a + 1)
                elif kind == "H":
                    pe.wait_ge(gelu_done, f * GELU_PER + 2 * (n + 1))
                elif kind == "GT":
                    pe.wait_ge(gateT_ready, f + 1)
                elif kind == "B1":
                    pe.wait_ge(b1_ready, 1)
                elif kind == "Y" and n // NT < NE:
                    pe.wait_ge(y_taken, f * NE + n // NT + 1)
                elif kind == "Y":
                    pe.wait_ge(out_ready, f + 1)
                elif kind == "T1":
                    pe.wait_ge(xnT_ready, bb + 1)
                elif kind == "QKV":
                    pe.wait_ge(qkv_free, bb + 1)
                elif kind == "TK":
                    pe.wait_ge(kst_ready, bb + 1)
                elif kind == "TQ":
                    pe.wait_ge(qst_ready, bb + 1)

            def run(b, phase):
                for (kind, n) in PHASES[phase]:
                    place, unit, when = PLACES[phase][kind, n]
                    if not (kind == "Y" and n % NT):
                        wait_read(b, unit, when)
                    if kind == "M":
                        max_scores(b, n, place)
                    elif kind == "E":
                        scores(b, n, place)
                    elif kind == "TM":
                        turn_maxima(b, n, place)
                    elif kind == "PV":
                        values(b, n)
                    elif kind == "TP":
                        turn_values(b, n, place)
                    elif kind == "TO":
                        turn_heads(b, place)
                    elif kind == "PJ":
                        project_out(b, place)
                    elif kind == "T2":
                        turn_x2(b, place)
                    elif kind == "RL":
                        logits(b)
                    elif kind == "H":
                        first_layer(b - 1, n, place)
                    elif kind == "Y":
                        second_layer(b - 1, n)
                    elif kind == "GT":
                        turn_gates(b - 1)
                    elif kind == "B1":
                        turn_biases()
                    elif kind == "T1":
                        turn_xn(b + 1, place)
                    elif kind == "QKV":
                        project(b + 1, place)
                    elif kind == "TK":
                        turn_stacks(b + 1, place, krows, k_spread, k_turned)
                    elif kind == "TQ":
                        turn_stacks(b + 1, place, qrows, q_spread, q_turned)

            pe.wait_ge(eyes_made, 1)
            run(-1, "prologue")
            pe.wait_ge(consts_made, 1)
            run(0, "first")
            pe.wait_ge(w1_split, NE + 1)
            run(1, "second")
            with pe.Fori(2, B - 1) as b:
                run(b, "loop")
            run(B - 1, "last")
            run(B, "experts")


_INS = ["L0_attn_x", "L0_attn_wq", "L0_attn_wk", "L0_attn_wv", "L0_attn_wo", "L0_attn_head_dirs", "L0_attn_scale",
        "L0_ffn_Wfc_s", "L0_ffn_bfc_s", "L0_ffn_Wproj_s", "L0_ffn_bproj_s", "L0_ffn_Wr", "L0_ffn_Wfc", "L0_ffn_bfc",
        "L0_ffn_Wproj", "L0_ffn_bproj"]


def kernel(**inputs):
    import numpy as _np
    import concourse.bacc as _bacc
    from concourse import mybir as _mybir
    from concourse.bass_utils import run_bass_kernel_spmd as _run

    nc = _bacc.Bacc("TRN2", target_bir_lowering=False, num_devices=1)
    arrays, args = {}, []
    for name in _INS:
        a = _np.ascontiguousarray(inputs[name])
        arrays[f"in_{name}"] = a
        args.append(nc.dram_tensor(f"in_{name}", a.shape, _mybir.dt.from_np(a.dtype), kind="ExternalInput").ap())
    args.append(nc.dram_tensor("out_0", (B, T, C), _mybir.dt.float32, kind="ExternalOutput").ap())
    attn_moe_kernel(nc, *args)
    r = _run(nc, [arrays], core_ids=[0])
    return r.results[0]["out_0"]
```
